# Optimizing a Trainium2 kernel written in Bass

```python
import numpy as np
import jax
import jax.numpy as jnp

def _softmax(x, axis=-1):
    return jax.nn.softmax(x, axis=axis)

def _gelu(x):
    return jax.nn.gelu(x, approximate=True)

def _silu(x):
    return jax.nn.silu(x)

def _sigmoid(x):
    return jax.nn.sigmoid(x)

def _layernorm(x, axis=-1, eps=1e-05):
    m = jnp.mean(x, axis=axis, keepdims=True)
    v = jnp.var(x, axis=axis, keepdims=True)
    return (x - m) / jnp.sqrt(v + eps)

def _scatter_add(tgt, idx, src, axis=0):
    return tgt.at[idx].add(src)

def _segment_sum(src, seg, n):
    return jax.ops.segment_sum(src, seg, n)
kernel_name = 'mk_xattn_ffn_d2_seqx_r8_ff1ddb'

def setup_inputs(seed: int=0):
    np.random.seed(seed)
    _w = jnp.asarray

    def _rec_inputs():
        import jax
        import jax.numpy as jnp
        _rk = jax.random.key(seed)
        x = 7.22e-05 + 1 * jax.random.normal(jax.random.fold_in(_rk, 1), (32, 64, 256), jnp.float32)
        _lenS = 64 - jax.random.randint(jax.random.fold_in(_rk, 7), (32,), 0, max(1, 64 // 4) + 1, jnp.int32)
        _lenS2 = 64 - jax.random.randint(jax.random.fold_in(_rk, 8), (32,), 0, max(1, 64 // 4) + 1, jnp.int32)
        _ctx_2048P = jax.random.normal(jax.random.fold_in(_rk, 11), (32, 16, 256), jnp.float32)
        _ctx_2048c = jax.random.dirichlet(jax.random.fold_in(_rk, 511), 0.3 * jnp.ones((16,), jnp.float32), (32, 64))
        _ctx_2048t = jnp.einsum('bsk,bkd->bsd', _ctx_2048c, _ctx_2048P)
        _ctx_2048t = _ctx_2048t * jax.lax.rsqrt(jnp.mean(jnp.square(_ctx_2048t)) + 1e-12) * 0.953939
        ctx_2048 = 4.13588e-05 + 0.999923 * (_ctx_2048t + 0.3 * jax.random.normal(jax.random.fold_in(_rk, 611), (32, 64, 256), jnp.float32))
        return (x, ctx_2048)
    x, ctx_2048 = _rec_inputs()

    def _L0_xattn_setup():
        import jax, jax.numpy as jnp
        import numpy as np
        B, S, DIM, HD = (4, 128, 256, 128)
        H = DIM // HD
        GN_EPS = 0.001

        def _decay_masks(n_heads, seq_len):
            gam = 1.0 - 2.0 ** (-5.0 - jnp.arange(n_heads, dtype=jnp.float32))
            idx = jnp.arange(seq_len, dtype=jnp.float32)
            expo = idx[None, :] - idx[:, None]
            D = jnp.where(expo[None, :, :] <= 0, gam[:, None, None] ** expo[None, :, :], 0.0)
            return D / jnp.sqrt(D.sum(axis=-1))[:, None, :]
        key = jax.random.key(seed)
        ks = jax.random.split(key, 8)
        x = jax.random.normal(ks[0], (B, S, DIM), dtype=jnp.float32)
        k = jax.random.normal(ks[1], (B, S, DIM), dtype=jnp.float32)
        v = jax.random.normal(ks[2], (B, S, DIM), dtype=jnp.float32)
        Wh = jax.random.normal(ks[3], (H, HD, HD), dtype=jnp.float32) / np.sqrt(HD)
        wg_w = jax.random.normal(ks[4], (DIM, DIM), dtype=jnp.float32) / np.sqrt(DIM)
        wo_w = jax.random.normal(ks[5], (DIM, DIM), dtype=jnp.float32) / np.sqrt(DIM)
        gn_gamma = jnp.ones((DIM,), dtype=jnp.float32)
        gn_beta = jnp.zeros((DIM,), dtype=jnp.float32)
        return {'x': x, 'k': k, 'v': v, 'Wh': Wh, 'wg_w': wg_w, 'wo_w': wo_w, 'gn_gamma': gn_gamma, 'gn_beta': gn_beta}
    _L0_xattn_all = _L0_xattn_setup()
    _L0_xattn_in = {k: v for k, v in _L0_xattn_all.items() if k in ('Wh', 'wg_w', 'wo_w', 'gn_gamma', 'gn_beta')}
    del _L0_xattn_all

    def _L0_ffn_setup():
        import jax, jax.numpy as jnp
        import numpy as np
        B, S, D = (2, 256, 256)
        MOE_D = 176
        E = 16
        K = 6
        ALPHA = 0.001

        def _moe_forward(x, gate_w, w_gate, w_up, w_down):
            b, s, d = x.shape
            T = b * s
            h = x.reshape(T, d)
            logits = h @ gate_w.T
            scores = jax.nn.softmax(logits.astype(jnp.float32), axis=-1)
            topk_w, topk_idx = jax.lax.top_k(scores, K)
            cw = jnp.zeros((T, E), jnp.float32)
            cw = cw.at[jnp.arange(T)[:, None], topk_idx].add(topk_w)
            y = jnp.zeros((T, d), x.dtype)
            for e in range(E):
                g = h @ w_gate[e].T
                u = h @ w_up[e].T
                out = jax.nn.silu(g) * u @ w_down[e].T
                y = y + cw[:, e:e + 1].astype(x.dtype) * out
            counts = jnp.sum(jax.nn.one_hot(topk_idx.reshape(b, s * K), E, dtype=jnp.float32), axis=1)
            ce = counts * (E / (s * K))
            scores_bse = scores.reshape(b, s, E)
            aux = jnp.mean(jnp.sum(ce * scores_bse.mean(axis=1), axis=1)) * ALPHA
            return (y.reshape(b, s, d), aux)
        key = jax.random.key(seed)
        ks = jax.random.split(key, 5)
        sd = 1.0 / np.sqrt(D)
        sm = 1.0 / np.sqrt(MOE_D)
        return {'x': jax.random.normal(ks[0], (B, S, D), jnp.float32), 'gate_w': jax.random.normal(ks[1], (E, D), jnp.float32) * sd, 'w_gate': jax.random.normal(ks[2], (E, MOE_D, D), jnp.float32) * sd, 'w_up': jax.random.normal(ks[3], (E, MOE_D, D), jnp.float32) * sd, 'w_down': jax.random.normal(ks[4], (E, D, MOE_D), jnp.float32) * sm}
    _L0_ffn_all = _L0_ffn_setup()
    _L0_ffn_in = {k: v for k, v in _L0_ffn_all.items() if k in ('gate_w', 'w_gate', 'w_up', 'w_down')}
    del _L0_ffn_all

    def _L1_xattn_setup():
        import math
        import jax, jax.numpy as jnp
        import numpy as np
        HEADS = 16
        MASKED_BIAS = -10000.0

        def _mha(q, k, v):
            B, Sq, D = q.shape
            Sk = k.shape[-2]
            hd = D // HEADS
            qh = q.reshape(B, Sq, HEADS, hd).transpose(0, 2, 1, 3)
            kh = k.reshape(B, Sk, HEADS, hd).transpose(0, 2, 1, 3)
            vh = v.reshape(B, Sk, HEADS, hd).transpose(0, 2, 1, 3)
            scores = jnp.einsum('bhqd,bhkd->bhqk', qh, kh) / math.sqrt(hd)
            qi = jnp.arange(Sq)[:, None] + (Sk - Sq)
            ki = jnp.arange(Sk)[None, :]
            causal = ki <= qi
            scores = jnp.where(causal[None, None], scores, jnp.asarray(MASKED_BIAS, scores.dtype))
            attn = jax.nn.softmax(scores, axis=-1)
            out = jnp.einsum('bhqk,bhkd->bhqd', attn, vh)
            return out.transpose(0, 2, 1, 3).reshape(B, Sq, D)
        key = jax.random.key(seed)
        kq, kk, kv = jax.random.split(key, 3)
        B, S, D = (4, 128, 256)
        q = jax.random.normal(kq, (B, S, D), dtype=jnp.float32)
        k = jax.random.normal(kk, (B, S, D), dtype=jnp.float32)
        v = jax.random.normal(kv, (B, S, D), dtype=jnp.float32)
        return {'q': q, 'k': k, 'v': v}
    _L1_xattn_all = _L1_xattn_setup()
    _L1_xattn_in = {k: v for k, v in _L1_xattn_all.items() if k in ()}
    del _L1_xattn_all

    def _L1_ffn_setup():
        import jax, jax.numpy as jnp
        import numpy as np
        H = 256
        I = 176
        E = 16
        G = 4
        TOPK_GROUP = 2
        K = 4
        SI = 2 * I
        SCALE = 1.0
        NORM = True
        B, S = (4, 64)

        def _swiglu(h):
            g, u = jnp.split(h, 2, axis=-1)
            return jax.nn.silu(g) * u

        def _combine_weights(xt, gate_w):
            T = xt.shape[0]
            scores = jax.nn.softmax(xt @ gate_w.T, axis=-1)
            group_scores = scores.reshape(T, G, E // G).max(axis=-1)
            _, gidx = jax.lax.top_k(group_scores, TOPK_GROUP)
            gmask = jnp.zeros((T, G), bool).at[jnp.arange(T)[:, None], gidx].set(True)
            emask = jnp.repeat(gmask, E // G, axis=1)
            masked = jnp.where(emask, scores, 0.0)
            w, eidx = jax.lax.top_k(masked, K)
            if NORM:
                w = w / (w.sum(-1, keepdims=True) + 1e-20)
            w = w * SCALE
            return jnp.zeros((T, E), xt.dtype).at[jnp.arange(T)[:, None], eidx].add(w)
        key = jax.random.key(seed)
        ks = jax.random.split(key, 6)
        sc = lambda fan_in: 1.0 / np.sqrt(fan_in)
        return {'x': jax.random.normal(ks[0], (B, S, H), jnp.float32), 'gate_w': jax.random.normal(ks[1], (E, H), jnp.float32) * sc(H), 'expert_up_w': jax.random.normal(ks[2], (E, 2 * I, H), jnp.float32) * sc(H), 'expert_down_w': jax.random.normal(ks[3], (E, H, I), jnp.float32) * sc(I), 'shared_up_w': jax.random.normal(ks[4], (2 * SI, H), jnp.float32) * sc(H), 'shared_down_w': jax.random.normal(ks[5], (H, SI), jnp.float32) * sc(SI)}
    _L1_ffn_all = _L1_ffn_setup()
    _L1_ffn_in = {k: v for k, v in _L1_ffn_all.items() if k in ('gate_w', 'expert_up_w', 'expert_down_w', 'shared_up_w', 'shared_down_w')}
    del _L1_ffn_all
    return {'x': x, 'ctx_2048': ctx_2048, 'L0_xattn_Wh': _L0_xattn_in['Wh'], 'L0_xattn_wg_w': _L0_xattn_in['wg_w'], 'L0_xattn_wo_w': _L0_xattn_in['wo_w'], 'L0_xattn_gn_gamma': _L0_xattn_in['gn_gamma'], 'L0_xattn_gn_beta': _L0_xattn_in['gn_beta'], 'L0_ffn_gate_w': _L0_ffn_in['gate_w'], 'L0_ffn_w_gate': _L0_ffn_in['w_gate'], 'L0_ffn_w_up': _L0_ffn_in['w_up'], 'L0_ffn_w_down': _L0_ffn_in['w_down'], 'L1_ffn_gate_w': _L1_ffn_in['gate_w'], 'L1_ffn_expert_up_w': _L1_ffn_in['expert_up_w'], 'L1_ffn_expert_down_w': _L1_ffn_in['expert_down_w'], 'L1_ffn_shared_up_w': _L1_ffn_in['shared_up_w'], 'L1_ffn_shared_down_w': _L1_ffn_in['shared_down_w']}

def reference(x, ctx_2048, L0_xattn_Wh, L0_xattn_wg_w, L0_xattn_wo_w, L0_xattn_gn_gamma, L0_xattn_gn_beta, L0_ffn_gate_w, L0_ffn_w_gate, L0_ffn_w_up, L0_ffn_w_down, L1_ffn_gate_w, L1_ffn_expert_up_w, L1_ffn_expert_down_w, L1_ffn_shared_up_w, L1_ffn_shared_down_w):
    import jax
    import jax.numpy as jnp

    def _L0_xattn_ref(x, k, v, Wh, wg_w, wo_w, gn_gamma, gn_beta):
        import jax, jax.numpy as jnp
        import numpy as np
        B, S, DIM, HD = (4, 128, 256, 128)
        H = DIM // HD
        GN_EPS = 0.001

        def _decay_masks(n_heads, seq_len):
            gam = 1.0 - 2.0 ** (-5.0 - jnp.arange(n_heads, dtype=jnp.float32))
            idx = jnp.arange(seq_len, dtype=jnp.float32)
            expo = idx[None, :] - idx[:, None]
            D = jnp.where(expo[None, :, :] <= 0, gam[:, None, None] ** expo[None, :, :], 0.0)
            return D / jnp.sqrt(D.sum(axis=-1))[:, None, :]
        b, s, dim = x.shape
        h, hd, _ = Wh.shape
        xh = x.reshape(b, s, h, hd)
        kh = k.reshape(b, s, h, hd)
        vh = v.reshape(b, s, h, hd)
        Q = jnp.einsum('bshd,hde->bshe', xh, Wh)
        K = jnp.einsum('bshd,hde->bshe', kh, Wh)
        V = jnp.einsum('bshd,hde->bshe', vh, Wh)
        scores = jnp.einsum('bshe,bthe->bhst', Q, K) / jnp.sqrt(jnp.float32(hd))
        Dn = _decay_masks(h, s)
        masked = scores * Dn[None, :, :, :]
        A = jnp.maximum(jnp.abs(masked.sum(axis=0)), 1.0)
        O = jnp.einsum('hst,bthe->bshe', A, V).reshape(b, s, dim)
        mu = O.mean(axis=-1, keepdims=True)
        var = O.var(axis=-1, keepdims=True)
        Y = (O - mu) / jnp.sqrt(var + GN_EPS) * gn_gamma + gn_beta
        W = jax.nn.relu(x @ wg_w)
        return W * Y @ wo_w

    def _L0_ffn_ref(x, gate_w, w_gate, w_up, w_down):
        import jax, jax.numpy as jnp
        import numpy as np
        B, S, D = (2, 256, 256)
        MOE_D = 176
        E = 16
        K = 6
        ALPHA = 0.001

        def _moe_forward(x, gate_w, w_gate, w_up, w_down):
            b, s, d = x.shape
            T = b * s
            h = x.reshape(T, d)
            logits = h @ gate_w.T
            scores = jax.nn.softmax(logits.astype(jnp.float32), axis=-1)
            topk_w, topk_idx = jax.lax.top_k(scores, K)
            cw = jnp.zeros((T, E), jnp.float32)
            cw = cw.at[jnp.arange(T)[:, None], topk_idx].add(topk_w)
            y = jnp.zeros((T, d), x.dtype)
            for e in range(E):
                g = h @ w_gate[e].T
                u = h @ w_up[e].T
                out = jax.nn.silu(g) * u @ w_down[e].T
                y = y + cw[:, e:e + 1].astype(x.dtype) * out
            counts = jnp.sum(jax.nn.one_hot(topk_idx.reshape(b, s * K), E, dtype=jnp.float32), axis=1)
            ce = counts * (E / (s * K))
            scores_bse = scores.reshape(b, s, E)
            aux = jnp.mean(jnp.sum(ce * scores_bse.mean(axis=1), axis=1)) * ALPHA
            return (y.reshape(b, s, d), aux)
        y, _aux = _moe_forward(x, gate_w, w_gate, w_up, w_down)
        return y

    def _L1_xattn_ref(q, k, v):
        import math
        import jax, jax.numpy as jnp
        import numpy as np
        HEADS = 16
        MASKED_BIAS = -10000.0

        def _mha(q, k, v):
            B, Sq, D = q.shape
            Sk = k.shape[-2]
            hd = D // HEADS
            qh = q.reshape(B, Sq, HEADS, hd).transpose(0, 2, 1, 3)
            kh = k.reshape(B, Sk, HEADS, hd).transpose(0, 2, 1, 3)
            vh = v.reshape(B, Sk, HEADS, hd).transpose(0, 2, 1, 3)
            scores = jnp.einsum('bhqd,bhkd->bhqk', qh, kh) / math.sqrt(hd)
            qi = jnp.arange(Sq)[:, None] + (Sk - Sq)
            ki = jnp.arange(Sk)[None, :]
            causal = ki <= qi
            scores = jnp.where(causal[None, None], scores, jnp.asarray(MASKED_BIAS, scores.dtype))
            attn = jax.nn.softmax(scores, axis=-1)
            out = jnp.einsum('bhqk,bhkd->bhqd', attn, vh)
            return out.transpose(0, 2, 1, 3).reshape(B, Sq, D)
        return _mha(q, k, v)

    def _L1_ffn_ref(x, gate_w, expert_up_w, expert_down_w, shared_up_w, shared_down_w):
        import jax, jax.numpy as jnp
        import numpy as np
        H = 256
        I = 176
        E = 16
        G = 4
        TOPK_GROUP = 2
        K = 4
        SI = 2 * I
        SCALE = 1.0
        NORM = True
        B, S = (4, 64)

        def _swiglu(h):
            g, u = jnp.split(h, 2, axis=-1)
            return jax.nn.silu(g) * u

        def _combine_weights(xt, gate_w):
            T = xt.shape[0]
            scores = jax.nn.softmax(xt @ gate_w.T, axis=-1)
            group_scores = scores.reshape(T, G, E // G).max(axis=-1)
            _, gidx = jax.lax.top_k(group_scores, TOPK_GROUP)
            gmask = jnp.zeros((T, G), bool).at[jnp.arange(T)[:, None], gidx].set(True)
            emask = jnp.repeat(gmask, E // G, axis=1)
            masked = jnp.where(emask, scores, 0.0)
            w, eidx = jax.lax.top_k(masked, K)
            if NORM:
                w = w / (w.sum(-1, keepdims=True) + 1e-20)
            w = w * SCALE
            return jnp.zeros((T, E), xt.dtype).at[jnp.arange(T)[:, None], eidx].add(w)
        Bq, Sq, _ = x.shape
        xt = x.reshape(-1, H)
        cw = _combine_weights(xt, gate_w)
        out = jnp.zeros_like(xt)
        for e in range(E):
            a = _swiglu(xt @ expert_up_w[e].T)
            out = out + cw[:, e:e + 1] * (a @ expert_down_w[e].T)
        out = out + _swiglu(xt @ shared_up_w.T) @ shared_down_w.T
        return out.reshape(Bq, Sq, H)
    x = x + _L0_xattn_ref(_layernorm(x, axis=-1), ctx_2048, ctx_2048, L0_xattn_Wh, L0_xattn_wg_w, L0_xattn_wo_w, L0_xattn_gn_gamma, L0_xattn_gn_beta)
    x = x + _L0_ffn_ref(_layernorm(x, axis=-1), L0_ffn_gate_w, L0_ffn_w_gate, L0_ffn_w_up, L0_ffn_w_down)
    x = x + _L1_xattn_ref(_layernorm(x, axis=-1), ctx_2048, ctx_2048)
    x = x + _L1_ffn_ref(_layernorm(x, axis=-1), L1_ffn_gate_w, L1_ffn_expert_up_w, L1_ffn_expert_down_w, L1_ffn_shared_up_w, L1_ffn_shared_down_w)
    return x

_drawn_inputs = setup_inputs


def setup_inputs(seed=0):
    import zlib

    import numpy as np

    out = dict(_drawn_inputs(seed))
    spreads = {'L0_xattn_gn_gamma': (1.0, 0.2), 'L0_xattn_gn_beta': (0.0, 0.1)}
    factors = {}
    for name, (base, spread) in spreads.items():
        noise = np.random.default_rng([zlib.crc32(name.encode()), seed]).standard_normal(out[name].shape)
        drawn = base * np.exp(spread * noise) if base else spread * noise
        out[name] = jnp.asarray(drawn.astype(out[name].dtype))
    for name, factor in factors.items():
        out[name] = (out[name] * factor).astype(out[name].dtype)
    return out
```

```python
from contextlib import ExitStack

import numpy as np

import concourse.bass as bass
from concourse import mybir

F32 = mybir.dt.float32
F32R = mybir.dt.float32r
BF16 = mybir.dt.bfloat16
ALU = mybir.AluOpType
ACT = mybir.ActivationFunctionType
AX = mybir.AxisListType.X

P = 128
B, S, D = 32, 64, 256
TOK = B * S
NT = TOK // P
DK = D // P
BLK = 512
NBLK = TOK // BLK
TPB = BLK // P
E = 16
HID = 176
SHARED = 352
NM = (E * HID // P, -(-(E * HID + SHARED) // P))
TOPK = (6, 4)
GROUPS, TOPG = 4, 2
HEADS, HD = 16, 16
RH = 2
PAIRS = HEADS // 2
VW = 2 * (HD + 1)
WCOLS = 3 * DK * P
LN_EPS, GN_EPS = 1e-5, 1e-3
MASKED = -10000.0
RAW, UNROLL = 4, 4


def retention_mixture_layers(nc, x_d, ctxT_d, ctxV_d, wh_d, wg_d, wo_d, gamma_d, beta_d, router_d,
                             w0_d, w1_d, sel_d, identf_d, identb_d, dmask_d, dup_d, par_d,
                             cbig_d, floor_d, out_d):
    w_d = (w0_d, w1_d)
    with ExitStack() as ctx:
        def sb(name, shape, dt=F32):
            return ctx.enter_context(nc.sbuf_tensor(name, shape, dt))

        def sem(name):
            return ctx.enter_context(nc.semaphore(name))

        x = sb("x", [P, NT, D])
        ident = sb("ident", [P, P])
        identb = sb("identb", [P, P], BF16)
        mean_var = sb("mean_var", [P, 4, NT, 2])
        var_eps = sb("var_eps", [P, 4, NT])
        rstd = sb("rstd", [P, 4, NT])
        minus_half = sb("minus_half", [P, NT])
        stats = sb("stats", [P, NT, 6])
        xn = sb("xn", [P, 2, D])
        x_hi = sb("x_hi", [P, DK, TOK], F32R)
        x_lo = sb("x_lo", [P, DK, TOK], F32R)
        big = sb("big", [P, 4 * TOK])
        xT = big[:, 0:DK * TOK].rearrange("p (k n) -> p k n", k=DK)
        qT = big[:, DK * TOK:2 * DK * TOK].rearrange("p (k n) -> p k n", k=DK)
        keys = big[:, :].rearrange("p (g a n) -> p g a n", g=DK, a=2)
        ctx_buf = sb("ctx_buf", [P, DK * TOK])
        ctxT = ctx_buf[:, :].rearrange("p (k n) -> p k n", k=DK)
        ctxV = ctx_buf[:, :].rearrange("p (b i d) -> p b i d", b=B, i=PAIRS)
        val_buf = sb("val_buf", [P, B * PAIRS * VW])
        kT = val_buf[:, 0:DK * TOK].rearrange("p (k n) -> p k n", k=DK)
        vals = val_buf[:, :].rearrange("p (b i w) -> p b i w", b=B, i=PAIRS)
        work = sb("work", [P, 8 * BLK])

        def pair_of(at, width):
            return work[:, at:at + 2 * width].rearrange("p (s n) -> p s n", s=2)

        vt, gate, gate_g, gate_b, yn, wy, wyT = (pair_of(2 * D * n, D) for n in range(7))
        sg, sgc, h = (pair_of(2 * BLK * n, BLK) for n in range(3))
        ysb = pair_of(6 * BLK, BLK)
        probs, probsT = (pair_of(4 * BLK * n, 2 * BLK) for n in range(2))
        free_at = [DK * TOK]

        def until_values(width):
            free_at[0] += width
            return val_buf[:, free_at[0] - width:free_at[0]]

        wh = until_values(RH * P).rearrange("p (h n) -> p h n", h=RH)
        wg = until_values(DK * D).rearrange("p (k n) -> p k n", k=DK)
        wo = until_values(DK * D).rearrange("p (k n) -> p k n", k=DK)
        gamma = until_values(D)
        beta = until_values(D)
        dmask = until_values(RH * S)[0:S]
        dup = until_values(P)[0:S]
        decayed = until_values(RH * S)[0:S]
        attn = until_values(RH * S)[0:S]
        attn_diag = until_values(RH * P).rearrange("p (h n) -> p h n", h=RH)
        gn_stats = sb("gn_stats", [P, 2, 6])
        gn_mv = sb("gn_mv", [P, 2, 2])
        gn_ve = sb("gn_ve", [P, 2])
        gn_rstd = sb("gn_rstd", [P, 2])
        parity = sb("parity", [P, 2])
        cbig = sb("cbig", [P, 4 * S], BF16)
        floor = sb("floor", [P, 4 * S])
        smax = sb("smax", [P, 2, HEADS])
        orec = sb("orec", [P, 2, HEADS])
        onorm = sb("onorm", [P, 2, D])
        q_t = sb("q_t", [P, 2, DK, P])
        router = sb("router", [P, 2 * DK * E])
        router_hi = sb("router_hi", [P, 2 * DK * E], F32R)
        router_lo = sb("router_lo", [P, 2 * DK * E], F32R)
        z = sb("z", [P, NT, E])
        ez = sb("ez", [P, NT, E])
        zmax = sb("zmax", [P, NT])
        zsum = sb("zsum", [P, NT])
        zrec = sb("zrec", [P, NT])
        cand = sb("cand", [P, NT, E + 4])
        left = sb("left", [P, NT, E + 4])
        top = sb("top", [P, NT, 8])
        gcand = sb("gcand", [P, NT, GROUPS + 8 - TOPG])
        gleft = sb("gleft", [P, NT, GROUPS + 8 - TOPG])
        gmask = sb("gmask", [P, NT, GROUPS])
        cw = sb("cw", [P, NT, E])
        cwp = sb("cwp", [P, NT, P], BF16)
        cwT = sb("cwT", [P, TOK], BF16)
        w_raw = sb("w_raw", [P, RAW, WCOLS])
        sel = sb("sel", [P, RAW, P], BF16)
        zero_col = sb("zero_col", [P, 1])
        zero = zero_col[:]
        w_hi = sb("w_hi", [P, 2, WCOLS], F32R)
        w_lo = sb("w_lo", [P, 2, WCOLS], F32R)
        h_hi = sb("h_hi", [P, 2, BLK], F32R)
        h_lo = sb("h_lo", [P, 2, BLK], F32R)

        psum = ctx.enter_context(nc.psum_tensor("psum", [P, 8, 512], F32))
        bank = [psum[:, i, :] for i in range(8)]
        tr_bank = bank[0:2]

        x_in = [sem(f"x_in{j}") for j in range(NBLK)]
        ident_in, consts_in, ctx_in, attw_in, vals_in = (sem(n) for n in ("ident_in", "consts_in", "ctx_in", "attw_in", "vals_in"))
        memset_done, var_ready, rstd_ready, xn_ready, tr_done, tr_hi, tr_evac = (
            sem(n) for n in ("memset_done", "var_ready", "rstd_ready", "xn_ready", "tr_done", "tr_hi", "tr_evac"))
        q_done, k_done, q_evac, k_evac, ret_scores, ret_attn, ret_dup, ret_diag = (
            sem(n) for n in ("q_done", "k_done", "q_evac", "k_evac", "ret_scores", "ret_attn", "ret_dup", "ret_diag"))
        v_done, v_evac, g_done, g_relu, gates_ready, o_done, gn_var, gn_ready, wy_ready, wyT_done, wyT_evac, \
            proj_done, x_added = (sem(n) for n in (
                "v_done", "v_evac", "g_done", "g_relu", "gates_ready", "o_done", "gn_var", "gn_ready", "wy_ready",
                "wyT_done", "wyT_evac", "proj_done", "x_added"))
        router_split, logits_done, z_ready, ez_ready, cwp_ready, cwT_done, cwT_evac = (
            sem(n) for n in ("router_split", "logits_done", "z_ready", "ez_ready", "cwp_ready", "cwT_done", "cwT_evac"))
        w_in = [sem(f"w_in{j}") for j in range(RAW)]
        up_split, down_split, gate_up_done, cw_done, up_done, down_done = (
            sem(n) for n in ("up_split", "down_split", "gate_up_done", "cw_done", "up_done", "down_done"))
        silu_ready, sgc_ready, h_ready, h_hi_ready, h_lo_ready, y_evac, yT_done, y_added = (
            sem(n) for n in ("silu_ready", "sgc_ready", "h_ready", "h_hi_ready", "h_lo_ready", "y_evac",
                             "yT_done", "y_added"))
        keys_ready, vals_ready, s_done, s_evac, smax_ready, shifted, probs_ready, pT_done, pT_act, pT_dve, \
            pv_done, att_added = (sem(n) for n in (
                "keys_ready", "vals_ready", "s_done", "s_evac", "smax_ready", "shifted", "probs_ready", "pT_done",
                "pT_act", "pT_dve", "pv_done", "att_added"))
        dve_chain, pool_chain, out_done = sem("dve_chain"), sem("pool_chain"), sem("out_done")

        STEPS = NBLK * sum(NM)

        def blocks(layer):
            return [(b, layer * NBLK * NM[0] + b * NM[layer]) for b in range(NBLK)]

        def over_steps(eng, layer, first, step):
            peel = NM[layer] % UNROLL
            peel += UNROLL if peel < RAW - 1 else 0
            for m in range(peel):
                step(first + m, m, first + m)
            with eng.Fori(0, (NM[layer] - peel) // UNROLL) as turn:
                for u in range(UNROLL):
                    m = turn * UNROLL + (peel + u)
                    step(m + first, m, first + peel + u)

        def at_least(eng, semaphore, value):
            if not isinstance(value, int) or value > 0:
                eng.wait_ge(semaphore, value)

        block = ctx.enter_context(nc.Block())

        @block.sync
        def _(sp):
            sp.dma_start(ident[:], identf_d).then_inc(ident_in, 16)
            for j in range(NBLK):
                sp.dma_start(x[:, TPB * j:TPB * (j + 1), :],
                             x_d[BLK * j:BLK * (j + 1), :].rearrange("(t p) d -> p t d", p=P)).then_inc(x_in[j], 16)
            sp.dma_start(wh, wh_d).then_inc(attw_in, 16)
            sp.dma_start(ctxT, ctxT_d).then_inc(ctx_in, 16)
            for dst, src in ((wg, wg_d), (wo, wo_d), (gamma, gamma_d), (beta, beta_d),
                             (dmask, dmask_d), (dup, dup_d)):
                sp.dma_start(dst, src).then_inc(attw_in, 16)
            for dst, src in ((identb[:], identb_d), (router[:], router_d), (parity[:], par_d), (cbig[:], cbig_d),
                             (floor[:], floor_d)):
                sp.dma_start(dst, src).then_inc(consts_in, 16)

            def store(b):
                sp.wait_ge(y_added, NBLK + b + 1)
                sp.dma_start(out_d[BLK * b:BLK * (b + 1), :].rearrange("(t p) d -> p t d", p=P),
                             x[:, TPB * b:TPB * (b + 1), :]).then_inc(out_done, 16)

            def load(n, m, s):
                at_least(sp, down_split, n - (RAW - 1))
                at_least(sp, cw_done, n - (RAW - 1))
                sp.dma_start(w_raw[:, s % RAW, :], w_of[m]).then_inc(w_in[s % RAW], 16)
                sp.dma_start(sel[:, s % RAW, :], sel_d[m]).then_inc(w_in[s % RAW], 16)

            for layer in range(2):
                w_of = w_d[layer]
                for b, first in blocks(layer):
                    over_steps(sp, layer, first, load)
                    if layer == 0 and b == 0:
                        sp.wait_ge(keys_ready, 1)
                        sp.dma_start(ctx_buf[:], ctxV_d).then_inc(vals_in, 16)
                    if layer == 1 and b > 0:
                        store(b - 1)
            store(NBLK - 1)
            sp.wait_ge(out_done, 16 * NBLK)

        @block.gpsimd
        def _(pool):
            count = [0]

            def chain(ins):
                count[0] += 1
                ins.then_inc(pool_chain, 1)
                pool.wait_ge(pool_chain, count[0])

            def norm_scale(ln, j):
                t = slice(TPB * j, TPB * (j + 1))
                pool.wait_ge(var_ready, NBLK * ln + j + 1)
                chain(pool.tensor_scalar(var_eps[:, ln, t], mean_var[:, ln, t, 1], LN_EPS, None, ALU.add))
                pool.tensor_tensor(rstd[:, ln, t], var_eps[:, ln, t], minus_half[:, t], ALU.pow).then_inc(rstd_ready, 1)

            chain(pool.memset(minus_half[:], -0.5))
            chain(pool.memset(zero, 0.0))
            pool.memset(attn_diag, 0.0).then_inc(memset_done, 1)
            for k in range(8 - TOPK[1]):
                pool.memset(cand[:, :, E + k:E + k + 1], 2.0 + k).then_inc(memset_done, 1)
            for k in range(8 - TOPG):
                pool.memset(gcand[:, :, GROUPS + k:GROUPS + k + 1], 2.0 + k).then_inc(memset_done, 1)
            chain(pool.memset(cwp[:], 0.0))
            pool.memset(cwp[:, :, 3 * E:3 * E + 1], 1.0).then_inc(memset_done, 1)
            for j in range(NBLK):
                norm_scale(0, j)
            pool.wait_ge(attw_in, 16 * 7)
            for t in range(NT):
                p = t % 2
                pool.wait_ge(g_relu, t + 1)
                at_least(pool, wy_ready, t - 1)
                pool.tensor_tensor(gate_g[:, p], gate[:, p], gamma, ALU.mult)
                pool.tensor_tensor(gate_b[:, p], gate[:, p], beta, ALU.mult).then_inc(gates_ready, 1)
                pool.wait_ge(gn_var, t + 1)
                chain(pool.tensor_scalar(gn_ve[:, p:p + 1], gn_mv[:, p, 1:2], GN_EPS, None, ALU.add))
                pool.tensor_tensor(gn_rstd[:, p:p + 1], gn_ve[:, p:p + 1], minus_half[:, 0:1],
                                   ALU.pow).then_inc(gn_ready, 1)
            for j in range(NBLK):
                norm_scale(1, j)
            pool.wait_ge(x_added, NT)
            pool.wait_ge(consts_in, 16 * 5)
            for g in range(DK):
                for a in range(2):
                    last = pool.tensor_scalar(keys[:, g, a, :], ctxT[:, g, :], parity[:, a:a + 1], None, ALU.mult)
            last.then_inc(keys_ready, 1)
            pool.memset(val_buf[:], 0.0).then_inc(pool_chain, 1)
            count[0] += 1
            pool.wait_ge(pool_chain, count[0])

            def split(n, m, s):
                q, r = s % 2, s % RAW
                raw, gu, dn = w_raw[:, r, :], slice(0, 2 * DK * P), slice(2 * DK * P, WCOLS)
                use = n - s % RAW
                pool.wait_ge(w_in[r], 32 + 8 * use)
                at_least(pool, up_done, n - 1)
                pool.tensor_tensor(w_hi[:, q, gu], raw[:, gu], zero.broadcast_to([P, 2 * DK * P]), ALU.add).then_inc(pool_chain, 1)
                pool.wait_ge(pool_chain, n * 2 + chain_base + 1)
                pool.tensor_tensor(w_lo[:, q, gu], raw[:, gu], w_hi[:, q, gu], ALU.subtract).then_inc(up_split, 1)
                at_least(pool, down_done, n - 1)
                pool.tensor_tensor(w_hi[:, q, dn], raw[:, dn], zero.broadcast_to([P, DK * P]), ALU.add).then_inc(pool_chain, 1)
                pool.wait_ge(pool_chain, n * 2 + chain_base + 2)
                pool.tensor_tensor(w_lo[:, q, dn], raw[:, dn], w_hi[:, q, dn], ALU.subtract).then_inc(down_split, 1)

            for layer in range(2):
                chain_base = count[0] - 2 * blocks(layer)[0][1]
                count[0] += 2 * NM[layer] * NBLK
                for b, first in blocks(layer):
                    over_steps(pool, layer, first, split)
                    if layer == 0 and b == 0:
                        pool.wait_ge(vals_in, 16)
                        pool.wait_ge(down_split, first + NM[0])
                        for a in range(2):
                            rows, at = slice(S * a, S * (a + 1)), a * (HD + 1)
                            pool.tensor_copy(vals[rows, :, :, at:at + HD], ctxV[rows]).then_inc(vals_ready, 1)
                            pool.wait_ge(vals_ready, 2 * a + 1)
                            pool.memset(vals[rows, :, :, at + HD:at + HD + 1], 1.0).then_inc(vals_ready, 1)
                            pool.wait_ge(vals_ready, 2 * a + 2)
                if layer == 0:
                    norm_scale(2, 0)
                    for t in range(NT):
                        if t % TPB == 0 and t // TPB + 1 < NBLK:
                            norm_scale(2, t // TPB + 1)
                        pool.wait_ge(smax_ready, t + 1)
                        sc = probs[:, t % 2].rearrange("p (h k) -> p h k", h=HEADS)
                        mx = smax[:, t % 2].unsqueeze(2).broadcast_to([P, HEADS, S])
                        pool.tensor_tensor(sc, sc, mx, ALU.subtract).then_inc(shifted, 1)
                    for j in range(NBLK):
                        norm_scale(3, j)

        @block.scalar
        def _(act):
            for t in range(NT):
                act.wait_ge(tr_done, t + 1)
                act.copy(xT[:, :, P * t:P * (t + 1)],
                         tr_bank[t % 2][:, 0:D].rearrange("p (k n) -> p k n", k=DK)).then_inc(tr_evac, 1)
            for n in range(RH * NBLK):
                hd, j = n // NBLK, n % NBLK
                act.wait_ge(q_done, n + 1)
                act.copy(qT[:, hd, BLK * j:BLK * (j + 1)], bank[2 + n % 2]).then_inc(q_evac, 1)
            for i in range(NT + 3):
                if i < NT:
                    act.wait_ge(v_done, i + 1)
                    at_least(act, o_done, i - 1)
                    act.copy(vt[:, i % 2], bank[i % 2][:, 0:D]).then_inc(v_evac, 1)
                    act.wait_ge(g_done, i + 1)
                    at_least(act, gates_ready, i - 1)
                    act.activation(gate[:, i % 2], bank[2 + i % 2][:, 0:D], ACT.Relu).then_inc(g_relu, 1)
                if i >= 3:
                    j = i - 3
                    act.wait_ge(wyT_done, j + 1)
                    at_least(act, proj_done, j - 1)
                    act.copy(wyT[:, j % 2], bank[4 + j % 2][:, 0:D]).then_inc(wyT_evac, 1)

            def mixture_input(layer):
                for t in range(NT):
                    act.wait_ge(tr_done, NT * (2 * layer + 1) + t + 1)
                    act.copy(x_hi[:, :, P * t:P * (t + 1)],
                             tr_bank[t % 2][:, 0:D].rearrange("p (k n) -> p k n", k=DK)).then_inc(tr_hi, 1)
                act.wait_ge(z_ready, layer + 1)
                act.activation(ez[:], z[:], ACT.Exp).then_inc(ez_ready, 1)
                for j in range(2):
                    act.wait_ge(cwT_done, 2 * layer + j + 1)
                    act.copy(cwT[:, TOK // 2 * j:TOK // 2 * (j + 1)],
                             bank[3 + j].bitcast(BF16)).then_inc(cwT_evac, 1)

            def step(n, m, s):
                q = s % 2
                act.wait_ge(gate_up_done, n + 1)
                at_least(act, sgc_ready, n - 1)
                act.activation(sg[:, q], bank[q], ACT.Silu).then_inc(silu_ready, 1)
                act.wait_ge(h_ready, n + 1)
                at_least(act, down_done, n - 1)
                act.copy(h_hi[:, q], h[:, q]).then_inc(h_hi_ready, 1)

            def mixture(layer):
                for b, first in blocks(layer):
                    over_steps(act, layer, first, step)
                    act.wait_ge(down_done, first + NM[layer])
                    at_least(act, yT_done, NBLK * layer + b)
                    act.copy(ysb, psum[:, 6:8, :]).then_inc(y_evac, 1)

            mixture_input(0)
            mixture(0)
            act.wait_ge(yT_done, NBLK)
            for i in range(NT + 1):
                if i < NT:
                    act.wait_ge(tr_done, 2 * NT + i + 1)
                    at_least(act, s_done, i - 1)
                    act.copy(q_t[:, i % 2], bank[0][:, 0:D].rearrange("p (k n) -> p k n", k=DK)) \
                       .then_inc(tr_evac, 1)
                if i >= 1:
                    j = i - 1
                    act.wait_ge(pT_done, j + 1)
                    at_least(act, pv_done, j - 1)
                    act.copy(probsT[:, j % 2, 0:BLK], bank[2]).then_inc(pT_act, 1)
                if i < NT:
                    act.wait_ge(shifted, i + 1)
                    act.activation(probs[:, i % 2], probs[:, i % 2], ACT.Exp).then_inc(probs_ready, 1)
            mixture_input(1)
            mixture(1)

        @block.vector
        def _(dve):
            count = [0]

            def chain(ins):
                count[0] += 1
                ins.then_inc(dve_chain, 1)
                dve.wait_ge(dve_chain, count[0])

            def norm_stats(ln, j):
                for t in range(TPB * j, TPB * (j + 1)):
                    last = dve.bn_stats(stats[:, t, :], x[:, t, :])
                chain(last)
                for t in range(TPB * j, TPB * (j + 1)):
                    last = dve.bn_aggr(mean_var[:, ln, t, :], stats[:, t, :])
                last.then_inc(var_ready, 1)

            def normalise(ln, t):
                if t % TPB == 0:
                    dve.wait_ge(rstd_ready, NBLK * ln + t // TPB + 1)
                at_least(dve, tr_done, NT * ln + t - 1)
                dve.tensor_scalar(xn[:, t % 2], x[:, t, :], mean_var[:, ln, t, 0:1], rstd[:, ln, t:t + 1],
                                  ALU.subtract, ALU.mult).then_inc(xn_ready, 1)

            for j in range(NBLK):
                dve.wait_ge(x_in[j], 16)
                norm_stats(0, j)
                if j > 0:
                    for t in range(TPB * (j - 1), TPB * j):
                        normalise(0, t)
            for t in range(NT - TPB, NT):
                normalise(0, t)
            for n in range(RH * NBLK):
                hd, j = n // NBLK, n % NBLK
                dve.wait_ge(k_done, n + 1)
                dve.tensor_copy(kT[:, hd, BLK * j:BLK * (j + 1)], bank[4 + n % 2]).then_inc(k_evac, 1)
            dve.wait_ge(ret_scores, 1)
            dve.wait_ge(attw_in, 16 * 7)
            chain(dve.tensor_tensor(decayed, bank[6][0:S, 0:RH * S], dmask, ALU.mult))
            chain(dve.scalar_tensor_tensor(out=attn, in0=decayed, scalar=-1.0, in1=decayed, op0=ALU.mult, op1=ALU.max))
            dve.tensor_scalar(attn, attn, 1.0, None, ALU.max).then_inc(ret_attn, 1)
            dve.wait_ge(ret_dup, 1)
            dve.wait_ge(memset_done, 1)
            for a in range(2):
                rows = slice(S * a, S * (a + 1))
                last = dve.tensor_copy(attn_diag[rows, :, rows],
                                       bank[7][rows, 0:RH * S].rearrange("p (h s) -> p h s", h=RH))
            last.then_inc(ret_diag, 1)
            for i in range(NT + 3):
                if i < NT:
                    p = i % 2
                    dve.wait_ge(o_done, i + 1)
                    chain(dve.bn_stats(gn_stats[:, p, :], bank[p][:, D:2 * D]))
                    at_least(dve, gn_ready, i - 1)
                    dve.bn_aggr(gn_mv[:, p, :], gn_stats[:, p, :]).then_inc(gn_var, 1)
                if 1 <= i <= NT:
                    j = i - 1
                    p = j % 2
                    dve.wait_ge(gn_ready, j + 1)
                    chain(dve.tensor_scalar(yn[:, p], bank[p][:, D:2 * D], gn_mv[:, p, 0:1], gn_rstd[:, p:p + 1],
                                            ALU.subtract, ALU.mult))
                    dve.wait_ge(gates_ready, j + 1)
                    at_least(dve, wyT_done, j - 1)
                    chain(dve.tensor_tensor(wy[:, p], yn[:, p], gate_g[:, p], ALU.mult))
                    dve.tensor_tensor(wy[:, p], wy[:, p], gate_b[:, p], ALU.add).then_inc(wy_ready, 1)
                if i >= 3:
                    j = i - 3
                    dve.wait_ge(proj_done, j + 1)
                    dve.tensor_tensor(x[:, j, :], x[:, j, :], bank[6 + j % 2][:, 0:D], ALU.add).then_inc(x_added, 1)

            def split_routers():
                chain(dve.tensor_copy(router_hi[:], router[:]))
                dve.tensor_tensor(router_lo[:], router[:], router_hi[:], ALU.subtract).then_inc(router_split, 1)

            def mixture_input(layer):
                ln = 2 * layer + 1

                def low(t):
                    dve.wait_ge(tr_hi, NT * layer + t + 1)
                    cols = slice(P * t, P * (t + 1))
                    dve.tensor_tensor(x_lo[:, :, cols], tr_bank[t % 2][:, 0:D].rearrange("p (k n) -> p k n", k=DK),
                                      x_hi[:, :, cols].bitcast(F32), ALU.subtract).then_inc(tr_evac, 1)

                norm_stats(ln, 0)
                for j in range(NBLK):
                    if j + 1 < NBLK:
                        norm_stats(ln, j + 1)
                    for t in range(TPB * j, TPB * (j + 1)):
                        normalise(ln, t)
                        if t >= 1:
                            low(t - 1)
                low(NT - 1)
                logits = bank[2][:, 0:NT * E].rearrange("p (t e) -> p t e", t=NT)

                def over(a, n=E):
                    return a.unsqueeze(2).broadcast_to([P, NT, n])

                dve.wait_ge(logits_done, layer + 1)
                chain(dve.tensor_reduce(zmax[:], logits, AX, ALU.max))
                dve.tensor_tensor(z[:], logits, over(zmax[:]), ALU.subtract).then_inc(z_ready, 1)
                dve.wait_ge(ez_ready, layer + 1)
                chain(dve.tensor_reduce(zsum[:], ez[:], AX, ALU.add))
                chain(dve.reciprocal(zrec[:], zsum[:]))
                scores = cand[:, :, 0:E]
                chain(dve.tensor_tensor(scores, ez[:], over(zrec[:]), ALU.mult))
                if layer == 1:
                    chain(dve.tensor_reduce(gcand[:, :, 0:GROUPS],
                                            scores.rearrange("p t (g e) -> p t g e", g=GROUPS), AX, ALU.max))
                    for t in range(NT):
                        last = dve.max(top[:, t, :], gcand[:, t, :])
                    chain(last)
                    for t in range(NT):
                        last = dve.match_replace(gleft[:, t, :], top[:, t, :], gcand[:, t, :], -1.0)
                    chain(last)
                    chain(dve.tensor_scalar(gmask[:], gleft[:, :, 0:GROUPS], 0.0, None, ALU.is_lt))
                    for g in range(GROUPS):
                        e = slice(g * E // GROUPS, (g + 1) * E // GROUPS)
                        last = dve.tensor_tensor(scores[:, :, e], scores[:, :, e],
                                                 over(gmask[:, :, g], E // GROUPS), ALU.mult)
                    chain(last)
                width = E + 8 - TOPK[layer]
                for t in range(NT):
                    last = dve.max(top[:, t, :], cand[:, t, 0:width])
                chain(last)
                for t in range(NT):
                    last = dve.match_replace(left[:, t, 0:width], top[:, t, :], cand[:, t, 0:width], 0.0)
                chain(last)
                chain(dve.tensor_tensor(cw[:], scores, left[:, :, 0:E], ALU.subtract))
                if layer == 1:
                    chain(dve.tensor_reduce(zsum[:], cw[:], AX, ALU.add))
                    chain(dve.tensor_scalar(zsum[:], zsum[:], 1e-20, None, ALU.add))
                    chain(dve.reciprocal(zrec[:], zsum[:]))
                    chain(dve.tensor_tensor(cw[:], cw[:], over(zrec[:]), ALU.mult))
                at_least(dve, cwT_done, 2 * layer)
                parts = [cwp[:, :, E * k:E * (k + 1)] for k in range(3)]
                chain(dve.tensor_copy(parts[0], cw[:]))
                chain(dve.tensor_tensor(z[:], cw[:], parts[0], ALU.subtract))
                chain(dve.tensor_copy(parts[1], z[:]))
                dve.tensor_tensor(parts[2], z[:], parts[1], ALU.subtract).then_inc(cwp_ready, 1)

            def step(n, m, s):
                q = s % 2
                dve.wait_ge(silu_ready, n + 1)
                dve.wait_ge(cw_done, n + 1)
                dve.tensor_tensor(sgc[:, q], sg[:, q], bank[4 + q], ALU.mult).then_inc(sgc_ready, 1)
                dve.wait_ge(up_done, n + 1)
                dve.wait_ge(sgc_ready, n + 1)
                dve.tensor_tensor(h[:, q], sgc[:, q], bank[2 + q], ALU.mult).then_inc(h_ready, 1)
                dve.wait_ge(h_hi_ready, n + 1)
                at_least(dve, down_done, n - 1)
                dve.tensor_tensor(h_lo[:, q], h[:, q], h_hi[:, q].bitcast(F32), ALU.subtract) \
                   .then_inc(h_lo_ready, 1)

            def mixture(layer):
                for b, first in blocks(layer):
                    over_steps(dve, layer, first, step)
                    dve.wait_ge(yT_done, NBLK * layer + b + 1)
                    xs = x[:, TPB * b:TPB * (b + 1), :].rearrange("p (k t) d -> p k (t d)", k=2)
                    dve.tensor_tensor(xs, xs, psum[:, 6:8, :], ALU.add).then_inc(y_added, 1)
                dve.wait_ge(y_added, NBLK * (layer + 1))

            dve.wait_ge(consts_in, 16 * 5)
            split_routers()
            dve.wait_ge(x_added, NT)
            dve.wait_ge(memset_done, 12)
            mixture_input(0)
            mixture(0)
            norm_stats(2, 0)
            for t in range(2):
                normalise(2, t)

            def heads(t):
                return probs[:, t % 2].rearrange("p (h k) -> p h k", h=HEADS)

            for i in range(NT + 1):
                if i < NT:
                    if i % TPB == 0 and i // TPB + 1 < NBLK:
                        norm_stats(2, i // TPB + 1)
                    dve.wait_ge(s_done, i + 1)
                    at_least(dve, pT_done, i - 1)
                    for g in range(DK):
                        dst = probs[:, i % 2].rearrange("p (g j n) -> p g j n", g=DK, j=4)[:, g]
                        src = psum[:, 4:8, g * 2 * S:(g + 1) * 2 * S]
                        fl = floor[:, 0:2 * S].unsqueeze(1).broadcast_to([P, 4, 2 * S])
                        last = dve.scalar_tensor_tensor(out=dst, in0=src, scalar=HD ** -0.5, in1=fl,
                                                        op0=ALU.mult, op1=ALU.max)
                    last.then_inc(s_evac, 1)
                    dve.wait_ge(s_evac, i + 1)
                    dve.tensor_reduce(smax[:, i % 2], heads(i), AX, ALU.max).then_inc(smax_ready, 1)
                    if i + 2 < NT:
                        normalise(2, i + 2)
                if i >= 1:
                    j = i - 1
                    dve.wait_ge(pT_done, j + 1)
                    at_least(dve, pv_done, j - 1)
                    dve.tensor_copy(probsT[:, j % 2, BLK:2 * BLK], bank[3]).then_inc(pT_dve, 1)
                    dve.wait_ge(pv_done, j + 1)
                    o = bank[1][:, 0:PAIRS * VW].rearrange("p (h w) -> p h w", w=HD + 1)
                    chain(dve.reciprocal(orec[:, j % 2], o[:, :, HD]))
                    chain(dve.tensor_tensor(onorm[:, j % 2].rearrange("p (h d) -> p h d", d=HD), o[:, :, 0:HD],
                                            orec[:, j % 2].unsqueeze(2).broadcast_to([P, HEADS, HD]), ALU.mult))
                    dve.tensor_tensor(x[:, j, :], x[:, j, :], onorm[:, j % 2], ALU.add).then_inc(att_added, 1)
            dve.wait_ge(att_added, NT)
            mixture_input(1)
            mixture(1)

        @block.tensor
        def _(pe):
            def transposes(ln, t):
                g = NT * ln + t
                one_bank = ln == 2
                pe.wait_ge(xn_ready, g + 1)
                at_least(pe, tr_evac, g if one_bank else g - 1)
                for k in range(DK):
                    last = pe.transpose(bank[0 if one_bank else t % 2][:, P * k:P * (k + 1)],
                                        xn[:, t % 2, P * k:P * (k + 1)], ident[:])
                last.then_inc(tr_done, 1)

            def three(out, a, b, start, stop):
                pe.matmul(out, a[0], b[0], start=start, stop=False)
                pe.matmul(out, a[0], b[1], start=False, stop=False)
                return pe.matmul(out, a[1], b[0], start=False, stop=stop)

            pe.wait_ge(ident_in, 16)
            for t in range(NT):
                transposes(0, t)
            pe.wait_ge(attw_in, 16 * 7)
            pe.wait_ge(ctx_in, 16)
            pe.wait_ge(tr_evac, NT)
            for n in range(RH * NBLK):
                hd, cols = n // NBLK, slice(BLK * (n % NBLK), BLK * (n % NBLK + 1))
                at_least(pe, q_evac, n - 1)
                pe.matmul(bank[2 + n % 2], wh[:, hd, :], xT[:, hd, cols], start=True, stop=True).then_inc(q_done, 1)
                at_least(pe, k_evac, n - 1)
                pe.matmul(bank[4 + n % 2], wh[:, hd, :], ctxT[:, hd, cols], start=True, stop=True).then_inc(k_done, 1)
            pe.wait_ge(q_evac, RH * NBLK)
            pe.wait_ge(k_evac, RH * NBLK)
            for hd in range(RH):
                for b in range(B):
                    seq = slice(S * b, S * (b + 1))
                    last = pe.matmul(bank[6][0:S, S * hd:S * (hd + 1)], kT[:, hd, seq], qT[:, hd, seq],
                                     start=b == 0, stop=b == B - 1)
            last.then_inc(ret_scores, 1)
            pe.wait_ge(ret_attn, 1)
            pe.matmul(bank[7][:, 0:RH * S], dup, attn, start=True, stop=True).then_inc(ret_dup, 1)
            for i in range(NT + 4):
                if 1 <= i <= NT:
                    p = (i - 1) % 2
                    pe.wait_ge(v_evac, i)
                    pe.wait_ge(ret_diag, 1)
                    for hd in range(RH):
                        last = pe.matmul(bank[p][:, D + P * hd:D + P * (hd + 1)], attn_diag[:, hd, :],
                                         vt[:, p, P * hd:P * (hd + 1)], start=True, stop=True)
                    last.then_inc(o_done, 1)
                if i < NT:
                    p, tile = i % 2, slice(P * i, P * (i + 1))
                    at_least(pe, wy_ready, i - 1)
                    for hd in range(RH):
                        last = pe.matmul(bank[p][:, P * hd:P * (hd + 1)], ctxT[:, hd, tile], wh[:, hd, :],
                                         start=True, stop=True)
                    last.then_inc(v_done, 1)
                    at_least(pe, g_relu, i - 1)
                    for k in range(DK):
                        last = pe.matmul(bank[2 + p][:, 0:D], xT[:, k, tile], wg[:, k, :], start=k == 0,
                                         stop=k == DK - 1)
                    last.then_inc(g_done, 1)
                if 3 <= i < NT + 3:
                    p = (i - 3) % 2
                    pe.wait_ge(wy_ready, i - 2)
                    at_least(pe, wyT_evac, i - 4)
                    for k in range(DK):
                        last = pe.transpose(bank[4 + p][:, P * k:P * (k + 1)], wy[:, p, P * k:P * (k + 1)], ident[:])
                    last.then_inc(wyT_done, 1)
                if 4 <= i:
                    p = (i - 4) % 2
                    pe.wait_ge(wyT_evac, i - 3)
                    at_least(pe, x_added, i - 5)
                    for k in range(DK):
                        last = pe.matmul(bank[6 + p][:, 0:D], wyT[:, p, P * k:P * (k + 1)], wo[:, k, :],
                                         start=k == 0, stop=k == DK - 1)
                    last.then_inc(proj_done, 1)

            def mixture_input(layer):
                ln = 2 * layer + 1

                def logits(t):
                    pe.wait_ge(tr_evac, NT * ln + t + 1)
                    tile = slice(P * t, P * (t + 1))
                    for k in range(DK):
                        e = slice((layer * DK + k) * E, (layer * DK + k + 1) * E)
                        last = three(bank[2][:, E * t:E * (t + 1)], (x_hi[:, k, tile], x_lo[:, k, tile]),
                                     (router_hi[:, e], router_lo[:, e]), k == 0, k == DK - 1)
                    return last

                pe.wait_ge(router_split, 1)
                for t in range(NT):
                    transposes(ln, t)
                    if t >= 1:
                        logits(t - 1)
                logits(NT - 1).then_inc(logits_done, 1)
                pe.wait_ge(cwp_ready, layer + 1)
                pe.wait_ge(consts_in, 16 * 5)
                half = NT // 2
                for j in range(2):
                    for t in range(half):
                        last = pe.transpose(bank[3 + j].bitcast(BF16)[:, P * t:P * (t + 1)],
                                            cwp[:, half * j + t, :], identb[:])
                    last.then_inc(cwT_done, 1)
                pe.wait_ge(cwT_evac, 2 * layer + 2)

            def mixture(layer):
                def sum_transposed(b):
                    pe.wait_ge(y_evac, NBLK * layer + b + 1)
                    for t in range(TPB):
                        for k in range(DK):
                            at = D * (t % 2) + P * k
                            last = pe.transpose(bank[6 + t // 2][:, at:at + P], ysb[:, k, P * t:P * (t + 1)], ident[:])
                    last.then_inc(yT_done, 1)

                for b, first in blocks(layer):
                    cols = slice(BLK * b, BLK * (b + 1))

                    def up(n, s):
                        q, r = s % 2, s % RAW
                        pe.wait_ge(up_split, n + 1)

                        def half(out, base):
                            for k in range(DK):
                                w = slice(base + P * k, base + P * (k + 1))
                                last = three(out, (w_hi[:, q, w], w_lo[:, q, w]),
                                             (x_hi[:, k, cols], x_lo[:, k, cols]), k == 0, k == DK - 1)
                            return last

                        at_least(pe, silu_ready, n - 1)
                        half(bank[q], 0).then_inc(gate_up_done, 1)
                        at_least(pe, sgc_ready, n - 1)
                        pe.matmul(bank[4 + q], sel[:, r, :], cwT[:, cols], start=True, stop=True).then_inc(cw_done, 1)
                        at_least(pe, h_ready, n - 1)
                        half(bank[2 + q], DK * P).then_inc(up_done, 1)

                    def down(n, s, start, stop):
                        q = s % 2
                        pe.wait_ge(down_split, n + 1)
                        pe.wait_ge(h_lo_ready, n + 1)
                        for k in range(DK):
                            w = slice(2 * DK * P + P * k, 2 * DK * P + P * (k + 1))
                            last = three(bank[6 + k], (w_hi[:, q, w], w_lo[:, q, w]), (h_hi[:, q], h_lo[:, q]),
                                         start, stop)
                        last.then_inc(down_done, 1)

                    def step(n, m, s):
                        up(n, s)
                        if isinstance(m, int) and m == 0:
                            if b > 0:
                                sum_transposed(b - 1)
                            return
                        if isinstance(m, int) and m == 1:
                            at_least(pe, y_added, NBLK * layer + b)
                        down(n - 1, s - 1, isinstance(m, int) and m == 1, False)

                    over_steps(pe, layer, first, step)
                    down(first + NM[layer] - 1, first + NM[layer] - 1, False, True)
                sum_transposed(NBLK - 1)

            mixture_input(0)
            mixture(0)
            transposes(2, 0)
            for i in range(NT + 1):
                if i < NT:
                    p = i % 2
                    pe.wait_ge(keys_ready, 1)
                    pe.wait_ge(tr_evac, 2 * NT + i + 1)
                    at_least(pe, s_evac, i)
                    for j in range(4):
                        pe.matmul(bank[4 + j][:, 0:4 * S], identb[:], cbig[:], start=True, stop=False,
                                  skip_group_check=True)
                    for b in range(2):
                        for g in range(DK):
                            for j in range(4):
                                rows, q = slice(32 * j, 32 * (j + 1)), slice(S * b, S * (b + 1))
                                seq = slice(S * (2 * i + b), S * (2 * i + b + 1))
                                last = pe.matmul(bank[4 + j][q, 2 * S * g:2 * S * (g + 1)], q_t[rows, p, g, q],
                                                 keys[rows, g, :, seq], start=False, stop=True,
                                                 skip_group_check=True)
                    last.then_inc(s_done, 1)
                    if i + 1 < NT:
                        transposes(2, i + 1)
                if i >= 1:
                    j = i - 1
                    p = j % 2
                    pe.wait_ge(probs_ready, j + 1)
                    at_least(pe, pT_act, j)
                    at_least(pe, pT_dve, j)
                    for n in range(PAIRS):
                        last = pe.transpose(bank[2 + n // 4][:, P * (n % 4):P * (n % 4 + 1)],
                                            probs[:, p, P * n:P * (n + 1)], ident[:])
                    last.then_inc(pT_done, 1)
                    pe.wait_ge(vals_ready, 4)
                    pe.wait_ge(pT_act, j + 1)
                    pe.wait_ge(pT_dve, j + 1)
                    at_least(pe, att_added, j)
                    for b in range(2):
                        for n in range(PAIRS):
                            q = slice(P * n + S * b, P * n + S * (b + 1))
                            last = pe.matmul(bank[1][S * b:S * (b + 1), VW * n:VW * (n + 1)], probsT[:, p, q],
                                             vals[:, 2 * j + b, n, :], start=True, stop=True)
                    last.then_inc(pv_done, 1)
            mixture_input(1)
            mixture(1)


def masks():
    f = np.float32
    gam = (1.0 - f(2.0) ** (-5.0 - np.arange(RH, dtype=f))).astype(f)
    at = np.arange(S, dtype=f)
    expo = at[None, :] - at[:, None]
    decay = np.where(expo[None] <= 0, gam[:, None, None] ** expo[None], 0.0).astype(f)
    decay = decay / np.sqrt(decay.sum(axis=-1, dtype=f))[:, None, :] / np.sqrt(f(P))
    dmask = np.ascontiguousarray(decay.transpose(2, 0, 1).reshape(S, RH * S), f)
    eye = np.eye(S, dtype=f)
    chan = np.arange(P)
    par = np.stack([(chan // HD % 2 == a) for a in range(2)], 1).astype(f)
    hidden = np.arange(NM[1] * P)
    owner = np.where(hidden < E * HID, hidden // HID, 3 * E)
    sel = np.zeros((NM[1], P, P), f)
    for k in range(3):
        rows = np.where(owner < E, owner + E * k, owner)
        sel[hidden // P, rows, hidden % P] = 1.0
    masked = np.arange(S)[None, :] > np.arange(S)[:, None]
    masked = np.tile(masked, (2, 4))
    return {
        "identf": np.eye(P, dtype=f), "identb": np.eye(P, dtype=f), "dmask": dmask, "dup": np.hstack([eye, eye]),
        "par": par, "sel": sel, "cbig": np.where(masked, f(-2.0 ** 100), f(0.0)).astype(f),
        "floor": np.where(masked, f(MASKED), f(-3.4e38)).astype(f),
    }


def slabs(gate, up, down):
    n = gate.shape[0] // P
    parts = [w.reshape(n, P, DK, P).transpose(0, 3, 2, 1).reshape(n, P, DK * P) for w in (gate, up)]
    return np.ascontiguousarray(np.concatenate(parts + [down.reshape(n, P, D)], 2))


def kernel(**inputs):
    import concourse.bacc as bacc
    import ml_dtypes
    from concourse.bass_utils import run_bass_kernel_spmd

    a = {k: np.asarray(v) for k, v in inputs.items()}
    c = masks()
    for k in ("identb", "sel", "cbig"):
        c[k] = c[k].astype(ml_dtypes.bfloat16)
    ctx = a["ctx_2048"]
    pad = np.zeros((NM[1] * P - E * HID - SHARED, D), np.float32)
    up1, sh1 = a["L1_ffn_expert_up_w"], a["L1_ffn_shared_up_w"]
    arrays = {
        "x": a["x"].reshape(TOK, D),
        "ctxT": ctx.reshape(TOK, DK, P).transpose(2, 1, 0),
        "ctxV": ctx.reshape(B, S, PAIRS, 2, HD).transpose(3, 1, 0, 2, 4).reshape(P, DK * TOK),
        "wh": a["L0_xattn_Wh"].transpose(1, 0, 2),
        "wg": a["L0_xattn_wg_w"].reshape(DK, P, D).transpose(1, 0, 2),
        "wo": a["L0_xattn_wo_w"].reshape(DK, P, D).transpose(1, 0, 2),
        "gamma": np.broadcast_to(a["L0_xattn_gn_gamma"], (P, D)),
        "beta": np.broadcast_to(a["L0_xattn_gn_beta"], (P, D)),
        "router": np.stack([a["L0_ffn_gate_w"], a["L1_ffn_gate_w"]]).reshape(2, E, DK, P).transpose(3, 0, 2, 1)
                    .reshape(P, 2 * DK * E),
        "w0": slabs(a["L0_ffn_w_gate"].reshape(-1, D), a["L0_ffn_w_up"].reshape(-1, D),
                    a["L0_ffn_w_down"].transpose(0, 2, 1).reshape(-1, D)),
        "w1": slabs(np.concatenate([up1[:, :HID].reshape(-1, D), sh1[:SHARED], pad]),
                    np.concatenate([up1[:, HID:].reshape(-1, D), sh1[SHARED:], pad]),
                    np.concatenate([a["L1_ffn_expert_down_w"].transpose(0, 2, 1).reshape(-1, D),
                                    a["L1_ffn_shared_down_w"].T, pad])),
        "sel": c["sel"], "identf": c["identf"], "identb": c["identb"], "dmask": c["dmask"], "dup": c["dup"],
        "par": c["par"], "cbig": c["cbig"], "floor": c["floor"],
    }
    arrays = {f"in_{k}": np.ascontiguousarray(v) for k, v in arrays.items()}
    nc = bacc.Bacc("TRN2", target_bir_lowering=False, num_devices=1)
    aps = [nc.dram_tensor(k, v.shape, mybir.dt.from_np(v.dtype), kind="ExternalInput").ap()
           for k, v in arrays.items()]
    out = nc.dram_tensor("out", (TOK, D), F32, kind="ExternalOutput").ap()
    retention_mixture_layers(nc, *aps, out)
    got = run_bass_kernel_spmd(nc, [arrays], core_ids=[0])
    return got.results[0]["out"].reshape(B, S, D)
```

```python
from contextlib import ExitStack

import numpy as np

import concourse.bass as bass
from concourse import mybir

F32 = mybir.dt.float32
F32R = mybir.dt.float32r
BF16 = mybir.dt.bfloat16
ALU = mybir.AluOpType
ACT = mybir.ActivationFunctionType
AX = mybir.AxisListType.X

P = 128
B, S, D = 32, 64, 256
TOK = B * S
NT = TOK // P
DK = D // P
BLK = 512
NBLK = TOK // BLK
TPB = BLK // P
E = 16
HID = 176
SHARED = 352
EXPERT_SLABS = E * HID // P
NM = (EXPERT_SLABS, -(-(E * HID + SHARED) // P))
ROWS = 16
HALF = P // ROWS
HALF_SLABS = HID // ROWS
TOPK = (6, 4)
GROUPS, TOPG = 4, 2
HEADS, HD = 16, 16
RH = 2
PAIRS = HEADS // 2
VW = 2 * (HD + 1)
WCOLS = 3 * DK * P
LN_EPS, GN_EPS = 1e-5, 1e-3
MASKED = -10000.0
RAW, UNROLL = 4, 4
PREP_STEPS = 13
STATS_FROM = 9
PREP_FROM = (8, 7)
PIECES = 2


def retention_mixture_layers(nc, x_d, ctxT_d, ctxV_d, wh_d, wg_d, wo_d, gamma_d, beta_d, router_d,
                             w0_d, w1_d, sel_d, identf_d, identb_d, dmask_d, dup_d, par_d,
                             cbig_d, floor_d, out_d):
    w_d = (w0_d, w1_d)
    with ExitStack() as ctx:
        def sb(name, shape, dt=F32):
            return ctx.enter_context(nc.sbuf_tensor(name, shape, dt))

        def sem(name):
            return ctx.enter_context(nc.semaphore(name))

        x = sb("x", [P, NT, D])
        ident = sb("ident", [P, P])
        identb = sb("identb", [P, P], BF16)
        mean_var = sb("mean_var", [P, 4, NT, 2])
        var_eps = sb("var_eps", [P, 4, NT])
        rstd = sb("rstd", [P, 4, NT])
        minus_half = sb("minus_half", [P, NT])
        stats = sb("stats", [P, NT, 6])
        xn = sb("xn", [P, 2, 2, D])
        x_hi = sb("x_hi", [P, 2, DK, BLK], F32R)
        x_lo = sb("x_lo", [P, 2, DK, BLK], F32R)
        big = sb("big", [P, 4 * TOK])
        xT = big[:, 0:DK * TOK].rearrange("p (k n) -> p k n", k=DK)
        qT = big[:, DK * TOK:2 * DK * TOK].rearrange("p (k n) -> p k n", k=DK)
        keys = big[:, :].rearrange("p (g a n) -> p g a n", g=DK, a=2)
        ctxT = sb("ctxT", [P, DK, TOK])
        ctxV = sb("ctxV", [P, B, PAIRS, HD])
        val_buf = sb("val_buf", [P, B * PAIRS * VW])
        kT = val_buf[:, 0:DK * TOK].rearrange("p (k n) -> p k n", k=DK)
        vals = val_buf[:, :].rearrange("p (b i w) -> p b i w", b=B, i=PAIRS)
        work = sb("work", [P, 8 * BLK])

        def pair_of(at, width):
            return work[:, at:at + 2 * width].rearrange("p (s n) -> p s n", s=2)

        vt, gate, gate_g, gate_b, yn, wy, wyT = (pair_of(2 * D * n, D) for n in range(7))
        sg, sgc, h = (pair_of(2 * BLK * n, BLK) for n in range(3))
        ysb = pair_of(6 * BLK, BLK)
        probs, probsT = (pair_of(4 * BLK * n, 2 * BLK) for n in range(2))
        free_at = [DK * TOK]

        def until_values(width):
            free_at[0] += width
            return val_buf[:, free_at[0] - width:free_at[0]]

        wh = until_values(RH * P).rearrange("p (h n) -> p h n", h=RH)
        wg = until_values(DK * D).rearrange("p (k n) -> p k n", k=DK)
        wo = until_values(DK * D).rearrange("p (k n) -> p k n", k=DK)
        gamma = until_values(D)
        beta = until_values(D)
        dmask = until_values(RH * S)[0:S]
        dup = until_values(P)[0:S]
        decayed = until_values(RH * S)[0:S]
        attn = until_values(RH * S)[0:S]
        attn_diag = until_values(RH * P).rearrange("p (h n) -> p h n", h=RH)
        gn_stats = sb("gn_stats", [P, 2, 6])
        gn_mv = sb("gn_mv", [P, 2, 2])
        gn_ve = sb("gn_ve", [P, 2])
        gn_rstd = sb("gn_rstd", [P, 2])
        parity = sb("parity", [P, 2])
        cbig = sb("cbig", [P, 4 * S], BF16)
        floor = sb("floor", [P, 4 * S])
        smax = sb("smax", [P, 2, HEADS])
        orec = sb("orec", [P, 2, HEADS])
        onorm = sb("onorm", [P, 2, D])
        q_t = sb("q_t", [P, 2, DK, P])
        router = sb("router", [P, 2 * DK * E])
        router_hi = sb("router_hi", [P, 2 * DK * E], F32R)
        router_lo = sb("router_lo", [P, 2 * DK * E], F32R)
        z = sb("z", [P, TPB, E])
        ez = sb("ez", [P, TPB, E])
        zmax = sb("zmax", [P, TPB])
        zsum = sb("zsum", [P, TPB])
        zrec = sb("zrec", [P, TPB])
        cand = sb("cand", [P, TPB, E + 4])
        left = sb("left", [P, TPB, E + 4])
        top = sb("top", [P, TPB, 8])
        gcand = sb("gcand", [P, TPB, GROUPS + 8 - TOPG])
        gleft = sb("gleft", [P, TPB, GROUPS + 8 - TOPG])
        gmask = sb("gmask", [P, TPB, GROUPS])
        cw = sb("cw", [P, TPB, E])
        cwp = sb("cwp", [P, TPB, P], BF16)
        cwT = sb("cwT", [P, BLK], BF16)
        weights = sb("weights", [P, 2, E // HALF, BLK])
        one = sb("one", [P, BLK])
        w_raw = sb("w_raw", [P, RAW, WCOLS])
        sel = sb("sel", [P, E // HALF, P], BF16)
        w_hi = sb("w_hi", [P, 2, WCOLS], F32R)
        w_lo = sb("w_lo", [P, 2, WCOLS], F32R)
        h_hi = sb("h_hi", [P, 2, BLK], F32R)
        h_lo = sb("h_lo", [P, 2, BLK], F32R)

        psum = ctx.enter_context(nc.psum_tensor("psum", [P, 8, 512], F32))
        bank = [psum[:, i, :] for i in range(8)]
        prep_bank = bank[5]

        def tr_bank(ln, t):
            if ln == 0:
                return bank[t % 2][:, 0:D]
            if ln == 2:
                return bank[0][:, 0:D]
            return bank[0][:, D:2 * D] if (ln, t // TPB) == (3, 0) else prep_bank[:, 0:D]

        def sum_bank(b):
            return psum[:, 6:8, :] if b + 1 < NBLK else psum[:, 2:4, :]

        def logits_at(ln, j):
            at = bank[1] if (ln, j) == (3, 0) else prep_bank
            return at[:, PAIRS * VW:PAIRS * VW + TPB * E].rearrange("p (t e) -> p t e", t=TPB)

        def cwT_at(ln, j):
            if (ln, j) == (3, 0):
                return bank[0].bitcast(BF16)[:, BLK:2 * BLK]
            return prep_bank.bitcast(BF16)[:, 0:BLK]

        x_in = [sem(f"x_in{j}") for j in range(NBLK)]
        ident_in, consts_in, ctx_in, attw_in, vals_in = (sem(n) for n in ("ident_in", "consts_in", "ctx_in", "attw_in", "vals_in"))
        var_ready, rstd_ready, xn_ready, tr_done, tr_evac = (
            [sem(f"{n}{ln}") for ln in range(4)]
            for n in ("var_ready", "rstd_ready", "xn_ready", "tr_done", "tr_evac"))
        memset_done, tr_hi = sem("memset_done"), sem("tr_hi")
        q_done, k_done, q_evac, k_evac, ret_scores, ret_attn, ret_dup, ret_diag = (
            sem(n) for n in ("q_done", "k_done", "q_evac", "k_evac", "ret_scores", "ret_attn", "ret_dup", "ret_diag"))
        v_done, v_evac, g_done, g_relu, gates_ready, o_done, gn_var, gn_ready, wy_ready, wyT_done, wyT_evac, \
            proj_done, x_added = (sem(n) for n in (
                "v_done", "v_evac", "g_done", "g_relu", "gates_ready", "o_done", "gn_var", "gn_ready", "wy_ready",
                "wyT_done", "wyT_evac", "proj_done", "x_added"))
        router_split, logits_done, z_ready, ez_ready, cwp_ready, cwT_done, cwT_evac, weights_done, weights_ready = (
            sem(n) for n in ("router_split", "logits_done", "z_ready", "ez_ready", "cwp_ready", "cwT_done", "cwT_evac",
                             "weights_done", "weights_ready"))
        w_in = [sem(f"w_in{j}") for j in range(RAW)]
        up_hi, down_hi, up_split, down_split, gate_done, up_done, down_done = (
            sem(n) for n in ("up_hi", "down_hi", "up_split", "down_split", "gate_done", "up_done", "down_done"))
        silu_ready, sgc_ready, h_ready, h_hi_ready, h_lo_ready, y_evac, yT_done, y_added = (
            sem(n) for n in ("silu_ready", "sgc_ready", "h_ready", "h_hi_ready", "h_lo_ready", "y_evac",
                             "yT_done", "y_added"))
        keys_ready, vals_clear, vals_ready, s_done, s_evac, smax_ready, shifted, probs_ready, pT_done, pT_act, pT_dve, \
            pv_done, att_added = (sem(n) for n in (
                "keys_ready", "vals_clear", "vals_ready", "s_done", "s_evac", "smax_ready", "shifted", "probs_ready", "pT_done",
                "pT_act", "pT_dve", "pv_done", "att_added"))
        dve_chain, pool_chain, out_done = sem("dve_chain"), sem("pool_chain"), sem("out_done")

        STEPS = NBLK * sum(NM)

        def blocks(layer):
            return [(b, layer * NBLK * NM[0] + b * NM[layer]) for b in range(NBLK)]

        def over_steps(eng, layer, first, step):
            turns = (EXPERT_SLABS - PREP_STEPS - 1) // UNROLL
            peel = EXPERT_SLABS - 1 - turns * UNROLL
            for m in range(peel):
                step(first + m, m, first + m)
            with eng.Fori(0, turns) as turn:
                for u in range(UNROLL):
                    m = turn * UNROLL + (peel + u)
                    step(m + first, m, first + peel + u)
            for m in range(EXPERT_SLABS - 1, NM[layer]):
                step(first + m, m, first + m)

        def piece_of(k):
            n = B // (PIECES * NBLK)
            return slice(n * k, n * (k + 1))

        def preparation(layer, b, m):
            return (2 * layer + 1, b + 1) if isinstance(m, int) and m < PREP_STEPS and b + 1 < NBLK else None

        def at_least(eng, semaphore, value):
            if not isinstance(value, int) or value > 0:
                eng.wait_ge(semaphore, value)

        block = ctx.enter_context(nc.Block())

        @block.sync
        def _(sp):
            sp.dma_start(ident[:], identf_d).then_inc(ident_in, 16)
            for j in range(NBLK):
                sp.dma_start(x[:, TPB * j:TPB * (j + 1), :],
                             x_d[BLK * j:BLK * (j + 1), :].rearrange("(t p) d -> p t d", p=P)).then_inc(x_in[j], 16)
            sp.dma_start(wh, wh_d).then_inc(attw_in, 16)
            sp.dma_start(ctxT[:], ctxT_d).then_inc(ctx_in, 16)
            for dst, src in ((wg, wg_d), (wo, wo_d), (gamma, gamma_d), (beta, beta_d),
                             (dmask, dmask_d), (dup, dup_d)):
                sp.dma_start(dst, src).then_inc(attw_in, 16)
            for dst, src in ((identb[:], identb_d), (sel[:], sel_d), (router[:], router_d), (parity[:], par_d), (cbig[:], cbig_d),
                             (floor[:], floor_d)):
                sp.dma_start(dst, src).then_inc(consts_in, 16)
            sp.dma_start(ctxV[:].rearrange("p b i d -> p (b i d)"), ctxV_d).then_inc(vals_in, 16)

            def store(b):
                sp.wait_ge(y_added, NBLK + b + 1)
                sp.dma_start(out_d[BLK * b:BLK * (b + 1), :].rearrange("(t p) d -> p t d", p=P),
                             x[:, TPB * b:TPB * (b + 1), :]).then_inc(out_done, 16)

            def load(n, m, s):
                at_least(sp, down_split, n - (RAW - 1))
                sp.dma_start(w_raw[:, s % RAW, :], w_of[m]).then_inc(w_in[s % RAW], 16)

            for layer in range(2):
                w_of = w_d[layer]
                for b, first in blocks(layer):
                    over_steps(sp, layer, first, load)
                    if layer == 1 and b > 0:
                        store(b - 1)
            store(NBLK - 1)
            sp.wait_ge(out_done, 16 * NBLK)

        @block.gpsimd
        def _(pool):
            count = [0]

            def chain(ins):
                count[0] += 1
                ins.then_inc(pool_chain, 1)
                pool.wait_ge(pool_chain, count[0])

            def norm_scale(ln, j):
                t = slice(TPB * j, TPB * (j + 1))
                pool.wait_ge(var_ready[ln], j + 1)
                chain(pool.tensor_scalar(var_eps[:, ln, t], mean_var[:, ln, t, 1], LN_EPS, None, ALU.add))
                pool.tensor_tensor(rstd[:, ln, t], var_eps[:, ln, t], minus_half[:, t], ALU.pow).then_inc(rstd_ready[ln], 1)

            chain(pool.memset(minus_half[:], -0.5))
            pool.memset(attn_diag, 0.0).then_inc(memset_done, 1)
            for k in range(8 - TOPK[1]):
                pool.memset(cand[:, :, E + k:E + k + 1], 2.0 + k).then_inc(memset_done, 1)
            for k in range(8 - TOPG):
                pool.memset(gcand[:, :, GROUPS + k:GROUPS + k + 1], 2.0 + k).then_inc(memset_done, 1)
            pool.memset(cwp[:], 0.0).then_inc(memset_done, 1)
            pool.memset(one[:], 1.0).then_inc(memset_done, 1)
            for j in range(NBLK):
                norm_scale(0, j)
            pool.wait_ge(attw_in, 16 * 7)
            for t in range(NT):
                p = t % 2
                if t in (PREP_FROM[0], PREP_FROM[0] + TPB):
                    norm_scale(1, (t - PREP_FROM[0]) // TPB)
                pool.wait_ge(g_relu, t + 1)
                at_least(pool, wy_ready, t - 1)
                pool.tensor_tensor(gate_g[:, p], gate[:, p], gamma, ALU.mult)
                pool.tensor_tensor(gate_b[:, p], gate[:, p], beta, ALU.mult).then_inc(gates_ready, 1)
                pool.wait_ge(gn_var, t + 1)
                chain(pool.tensor_scalar(gn_ve[:, p:p + 1], gn_mv[:, p, 1:2], GN_EPS, None, ALU.add))
                pool.tensor_tensor(gn_rstd[:, p:p + 1], gn_ve[:, p:p + 1], minus_half[:, 0:1],
                                   ALU.pow).then_inc(gn_ready, 1)

            def split_up(n, s):
                q, r, up = s % 2, s % RAW, slice(0, 2 * DK * P)
                pool.wait_ge(up_hi, n + 1)
                pool.tensor_tensor(w_lo[:, q, up], w_raw[:, r, up], w_hi[:, q, up], ALU.subtract) \
                    .then_inc(up_split, 1)

            def split_down(n, s):
                q, r, down = s % 2, s % RAW, slice(2 * DK * P, WCOLS)
                pool.wait_ge(down_hi, n + 1)
                pool.tensor_tensor(w_lo[:, q, down], w_raw[:, r, down], w_hi[:, q, down], ALU.subtract) \
                    .then_inc(down_split, 1)

            def values_piece(b, k):
                a, piece = k % 2, PIECES * b + k // 2
                rows, at, seqs = slice(S * a, S * (a + 1)), a * (HD + 1), piece_of(piece)
                pool.wait_ge(vals_clear, piece + 1)
                pool.wait_ge(vals_in, 16)
                pool.tensor_copy(vals[rows, seqs, :, at:at + HD], ctxV[rows, seqs]).then_inc(vals_ready, 1)
                pool.wait_ge(vals_ready, 2 * PIECES * b + k + 1)

            split_up(0, 0)
            for layer in range(2):
                for b, first in blocks(layer):
                    def step(n, m, s):
                        if not (isinstance(n, int) and n == STEPS - 1):
                            split_up(n + 1, s + 1)
                        split_down(n, s)
                        if isinstance(m, int) and m == STATS_FROM + TPB - 1 and b + 2 < NBLK:
                            norm_scale(2 * layer + 1, b + 2)
                        if layer == 0 and isinstance(m, int) and 8 <= m < 8 + 2 * PIECES:
                            pool.wait_ge(down_split, n + 1)
                            values_piece(b, m - 8)

                    over_steps(pool, layer, first, step)
                if layer == 0:
                    norm_scale(2, 0)
                    for t in range(NT):
                        if t % TPB == 0 and t // TPB + 1 < NBLK:
                            norm_scale(2, t // TPB + 1)
                        if t in (PREP_FROM[1], PREP_FROM[1] + TPB):
                            norm_scale(3, (t - PREP_FROM[1]) // TPB)
                        pool.wait_ge(smax_ready, t + 1)
                        sc = probs[:, t % 2].rearrange("p (h k) -> p h k", h=HEADS)
                        mx = smax[:, t % 2].unsqueeze(2).broadcast_to([P, HEADS, S])
                        pool.tensor_tensor(sc, sc, mx, ALU.subtract).then_inc(shifted, 1)

        @block.scalar
        def _(act):
            def high(ln, t):
                act.wait_ge(tr_done[ln], t + 1)
                cols = slice(P * (t % TPB), P * (t % TPB + 1))
                act.copy(x_hi[:, t // TPB % 2, :, cols],
                         tr_bank(ln, t).rearrange("p (k n) -> p k n", k=DK)).then_inc(tr_hi, 1)

            def router_exp(ln, j):
                act.wait_ge(z_ready, NBLK * (ln // 2) + j + 1)
                act.activation(ez[:], z[:], ACT.Exp).then_inc(ez_ready, 1)

            def combine_weights(ln, j):
                act.wait_ge(cwT_done, NBLK * (ln // 2) + j + 1)
                at_least(act, weights_done, NBLK * (ln // 2) + j)
                act.copy(cwT[:], cwT_at(ln, j)).then_inc(cwT_evac, 1)

            def spread_weights(ln, j):
                act.wait_ge(weights_done, NBLK * (ln // 2) + j + 1)
                act.copy(weights[:, j % 2], psum[:, 4:6, :]).then_inc(weights_ready, 1)

            def prepare(ln, j, m):
                if 1 <= m < 1 + TPB:
                    high(ln, TPB * j + m - 1)
                if m == 5:
                    router_exp(ln, j)
                if m == 11:
                    combine_weights(ln, j)
                if m == 12:
                    spread_weights(ln, j)

            def prepare_rest(ln):
                for m in range(11, PREP_STEPS):
                    prepare(ln, 0, m)

            def up_high(n, s):
                q, r, up = s % 2, s % RAW, slice(0, 2 * DK * P)
                act.wait_ge(w_in[r], (n - r) * (16 // RAW) + 16)
                at_least(act, up_done, n - 1)
                act.copy(w_hi[:, q, up], w_raw[:, r, up]).then_inc(up_hi, 1)

            for t in range(NT):
                act.wait_ge(tr_done[0], t + 1)
                act.copy(xT[:, :, P * t:P * (t + 1)],
                         tr_bank(0, t).rearrange("p (k n) -> p k n", k=DK)).then_inc(tr_evac[0], 1)
            for n in range(RH * NBLK):
                hd, j = n // NBLK, n % NBLK
                act.wait_ge(q_done, n + 1)
                act.copy(qT[:, hd, BLK * j:BLK * (j + 1)], bank[2 + n % 2]).then_inc(q_evac, 1)
            for i in range(NT + 3):
                if i < NT:
                    act.wait_ge(v_done, i + 1)
                    at_least(act, o_done, i - 1)
                    act.copy(vt[:, i % 2], bank[3][:, 0:D]).then_inc(v_evac, 1)
                    act.wait_ge(g_done, i + 1)
                    at_least(act, gates_ready, i - 1)
                    act.activation(gate[:, i % 2], bank[2][:, 0:D], ACT.Relu).then_inc(g_relu, 1)
                if i >= 3:
                    j = i - 3
                    act.wait_ge(wyT_done, j + 1)
                    at_least(act, proj_done, j - 1)
                    act.copy(wyT[:, j % 2], bank[4][:, 0:D]).then_inc(wyT_evac, 1)
                if PREP_FROM[0] < i:
                    prepare(1, 0, i - PREP_FROM[0] - 1)
                if i == NT // 2:
                    up_high(0, 0)

            def keys_piece(b, k):
                g, a, cols = k // 2, k % 2, slice(BLK * b, BLK * (b + 1))
                act.activation(keys[:, g, a, cols], ctxT[:, g, cols], ACT.Copy,
                               scale=parity[:, a:a + 1]).then_inc(keys_ready, 1)

            def mixture(layer):
                def sum_to_sbuf(b, through):
                    act.wait_ge(down_done, through)
                    at_least(act, yT_done, NBLK * layer + b)
                    act.copy(ysb, psum[:, 6:8, :]).then_inc(y_evac, 1)

                for b, first in blocks(layer):
                    def step(n, m, s):
                        q, r, down = s % 2, s % RAW, slice(2 * DK * P, WCOLS)
                        if isinstance(m, int) and m == 1 and b > 0:
                            sum_to_sbuf(b - 1, first)
                        if not (isinstance(n, int) and n == STEPS - 1):
                            up_high(n + 1, s + 1)
                        act.wait_ge(gate_done, n + 1)
                        at_least(act, sgc_ready, n - 1)
                        act.activation(sg[:, q], bank[q], ACT.Silu).then_inc(silu_ready, 1)
                        at_least(act, down_done, n - 1)
                        act.copy(w_hi[:, q, down], w_raw[:, r, down]).then_inc(down_hi, 1)
                        act.wait_ge(h_ready, n + 1)
                        act.copy(h_hi[:, q], h[:, q]).then_inc(h_hi_ready, 1)
                        if preparation(layer, b, m):
                            prepare(*preparation(layer, b, m), m)
                        if layer == 0 and isinstance(m, int) and 7 <= m < 11:
                            keys_piece(b, m - 7)

                    over_steps(act, layer, first, step)
                sum_to_sbuf(NBLK - 1, first + NM[layer])

            prepare_rest(1)
            mixture(0)
            act.wait_ge(yT_done, NBLK)

            def queries(t):
                act.wait_ge(tr_done[2], t + 1)
                at_least(act, s_done, t - 1)
                act.copy(q_t[:, t % 2], tr_bank(2, t).rearrange("p (k n) -> p k n", k=DK)).then_inc(tr_evac[2], 1)

            queries(0)
            for i in range(NT + 2):
                if i >= 2:
                    j = i - 2
                    act.wait_ge(pT_done, j + 1)
                    at_least(act, pv_done, j - 1)
                    act.copy(probsT[:, j % 2, 0:BLK], bank[2]).then_inc(pT_act, 1)
                if 1 <= i <= NT:
                    act.wait_ge(shifted, i)
                    act.activation(probs[:, (i - 1) % 2], probs[:, (i - 1) % 2], ACT.Exp).then_inc(probs_ready, 1)
                if i + 1 < NT:
                    queries(i + 1)
                if PREP_FROM[1] <= i:
                    prepare(3, 0, i - PREP_FROM[1])
            prepare_rest(3)
            mixture(1)

        @block.vector
        def _(dve):
            count = [0]

            def chain(ins):
                count[0] += 1
                ins.then_inc(dve_chain, 1)
                dve.wait_ge(dve_chain, count[0])

            def norm_stats(ln, j):
                for t in range(TPB * j, TPB * (j + 1)):
                    last = dve.bn_stats(stats[:, t, :], x[:, t, :])
                chain(last)
                for t in range(TPB * j, TPB * (j + 1)):
                    last = dve.bn_aggr(mean_var[:, ln, t, :], stats[:, t, :])
                last.then_inc(var_ready[ln], 1)

            def tile_stats(ln, t):
                chain(dve.bn_stats(stats[:, t, :], x[:, t, :]))
                last = dve.bn_aggr(mean_var[:, ln, t, :], stats[:, t, :])
                if t % TPB == TPB - 1:
                    last.then_inc(var_ready[ln], 1)

            def normalise(ln, t):
                if t % TPB == 0:
                    dve.wait_ge(rstd_ready[ln], t // TPB + 1)
                at_least(dve, tr_done[ln], t - 1)
                dve.tensor_scalar(xn[:, ln % 2, t % 2], x[:, t, :], mean_var[:, ln, t, 0:1], rstd[:, ln, t:t + 1],
                                  ALU.subtract, ALU.mult).then_inc(xn_ready[ln], 1)

            def split_routers():
                chain(dve.tensor_copy(router_hi[:], router[:]))
                dve.tensor_tensor(router_lo[:], router[:], router_hi[:], ALU.subtract).then_inc(router_split, 1)

            def low(ln, t):
                dve.wait_ge(tr_hi, NT * (ln // 2) + t + 1)
                part, cols = t // TPB % 2, slice(P * (t % TPB), P * (t % TPB + 1))
                dve.tensor_tensor(x_lo[:, part, :, cols], tr_bank(ln, t).rearrange("p (k n) -> p k n", k=DK),
                                  x_hi[:, part, :, cols].bitcast(F32), ALU.subtract).then_inc(tr_evac[ln], 1)

            def over(a, n=E):
                return a.unsqueeze(2).broadcast_to([P, TPB, n])

            def router_shift(ln, j):
                dve.wait_ge(logits_done, NBLK * (ln // 2) + j + 1)
                chain(dve.tensor_reduce(zmax[:], logits_at(ln, j), AX, ALU.max))
                dve.tensor_tensor(z[:], logits_at(ln, j), over(zmax[:]), ALU.subtract).then_inc(z_ready, 1)

            scores = cand[:, :, 0:E]

            def router_softmax(ln, j):
                layer = ln // 2
                dve.wait_ge(ez_ready, NBLK * layer + j + 1)
                chain(dve.tensor_reduce(zsum[:], ez[:], AX, ALU.add))
                chain(dve.reciprocal(zrec[:], zsum[:]))
                chain(dve.tensor_tensor(scores, ez[:], over(zrec[:]), ALU.mult))

            def router_groups(ln, j):
                if ln // 2 == 1:
                    chain(dve.tensor_reduce(gcand[:, :, 0:GROUPS],
                                            scores.rearrange("p t (g e) -> p t g e", g=GROUPS), AX, ALU.max))
                    for t in range(TPB):
                        last = dve.max(top[:, t, :], gcand[:, t, :])
                    chain(last)
                    for t in range(TPB):
                        last = dve.match_replace(gleft[:, t, :], top[:, t, :], gcand[:, t, :], -1.0)
                    chain(last)
                    chain(dve.tensor_scalar(gmask[:], gleft[:, :, 0:GROUPS], 0.0, None, ALU.is_lt))
                    for g in range(GROUPS):
                        e = slice(g * E // GROUPS, (g + 1) * E // GROUPS)
                        last = dve.tensor_tensor(scores[:, :, e], scores[:, :, e],
                                                 over(gmask[:, :, g], E // GROUPS), ALU.mult)
                    chain(last)

            def router_choose(ln, j):
                layer = ln // 2
                width = E + 8 - TOPK[layer]
                for t in range(TPB):
                    last = dve.max(top[:, t, :], cand[:, t, 0:width])
                chain(last)
                for t in range(TPB):
                    last = dve.match_replace(left[:, t, 0:width], top[:, t, :], cand[:, t, 0:width], 0.0)
                chain(last)
                chain(dve.tensor_tensor(cw[:], scores, left[:, :, 0:E], ALU.subtract))

            def router_norm(ln, j):
                if ln // 2 == 1:
                    chain(dve.tensor_reduce(zsum[:], cw[:], AX, ALU.add))
                    chain(dve.tensor_scalar(zsum[:], zsum[:], 1e-20, None, ALU.add))
                    chain(dve.reciprocal(zrec[:], zsum[:]))
                    chain(dve.tensor_tensor(cw[:], cw[:], over(zrec[:]), ALU.mult))

            def router_parts(ln, j):
                at_least(dve, cwT_done, NBLK * (ln // 2) + j)
                parts = [cwp[:, :, E * k:E * (k + 1)] for k in range(3)]
                chain(dve.tensor_copy(parts[0], cw[:]))
                chain(dve.tensor_tensor(z[:], cw[:], parts[0], ALU.subtract))
                chain(dve.tensor_copy(parts[1], z[:]))
                dve.tensor_tensor(parts[2], z[:], parts[1], ALU.subtract).then_inc(cwp_ready, 1)

            router_stages = (router_softmax, router_groups, router_choose, router_norm, router_parts)

            def prepare(ln, j, m):
                if 1 <= m < 1 + TPB:
                    low(ln, TPB * j + m - 1)
                if m < TPB:
                    normalise(ln, TPB * j + m)
                if m == 5:
                    router_shift(ln, j)
                for at, stage in enumerate(router_stages):
                    if m == 6 + at:
                        stage(ln, j)

            for j in range(NBLK):
                dve.wait_ge(x_in[j], 16)
                norm_stats(0, j)
                if j > 0:
                    for t in range(TPB * (j - 1), TPB * j):
                        normalise(0, t)
            for t in range(NT - TPB, NT):
                normalise(0, t)
            for n in range(RH * NBLK):
                hd, j = n // NBLK, n % NBLK
                dve.wait_ge(k_done, n + 1)
                dve.tensor_copy(kT[:, hd, BLK * j:BLK * (j + 1)], bank[4 + n % 2]).then_inc(k_evac, 1)
            dve.wait_ge(consts_in, 16 * 6)
            split_routers()
            dve.wait_ge(memset_done, 13)
            dve.wait_ge(ret_scores, 1)
            dve.wait_ge(attw_in, 16 * 7)
            chain(dve.tensor_tensor(decayed, bank[6][0:S, 0:RH * S], dmask, ALU.mult))
            chain(dve.scalar_tensor_tensor(out=attn, in0=decayed, scalar=-1.0, in1=decayed, op0=ALU.mult, op1=ALU.max))
            dve.tensor_scalar(attn, attn, 1.0, None, ALU.max).then_inc(ret_attn, 1)
            dve.wait_ge(ret_dup, 1)
            for a in range(2):
                rows = slice(S * a, S * (a + 1))
                last = dve.tensor_copy(attn_diag[rows, :, rows],
                                       bank[7][rows, 0:RH * S].rearrange("p (h s) -> p h s", h=RH))
            last.then_inc(ret_diag, 1)
            for i in range(NT + 3):
                if 1 <= i <= NT:
                    j = i - 1
                    p = j % 2
                    dve.wait_ge(gn_ready, j + 1)
                    chain(dve.tensor_scalar(yn[:, p], bank[p][:, 0:D], gn_mv[:, p, 0:1], gn_rstd[:, p:p + 1],
                                            ALU.subtract, ALU.mult))
                    dve.wait_ge(gates_ready, j + 1)
                    at_least(dve, wyT_done, j - 1)
                    chain(dve.tensor_tensor(wy[:, p], yn[:, p], gate_g[:, p], ALU.mult))
                    dve.tensor_tensor(wy[:, p], wy[:, p], gate_b[:, p], ALU.add).then_inc(wy_ready, 1)
                if i < NT:
                    p = i % 2
                    dve.wait_ge(o_done, i + 1)
                    chain(dve.bn_stats(gn_stats[:, p, :], bank[p][:, 0:D]))
                    at_least(dve, gn_ready, i - 1)
                    dve.bn_aggr(gn_mv[:, p, :], gn_stats[:, p, :]).then_inc(gn_var, 1)
                if i >= 3:
                    j = i - 3
                    dve.wait_ge(proj_done, j + 1)
                    dve.tensor_tensor(x[:, j, :], x[:, j, :], bank[6 + j % 2][:, 0:D], ALU.add).then_inc(x_added, 1)
                if PREP_FROM[0] - TPB <= i < PREP_FROM[0] + TPB:
                    dve.wait_ge(x_added, i - 3)
                    tile_stats(1, i - (PREP_FROM[0] - TPB))
                if PREP_FROM[0] <= i:
                    prepare(1, 0, i - PREP_FROM[0])

            def clear_values(piece):
                seqs = piece_of(piece)
                chain(dve.memset(vals[:, seqs], 0.0))
                for a in range(2):
                    rows, at = slice(S * a, S * (a + 1)), a * (HD + 1) + HD
                    last = dve.memset(vals[rows, seqs, :, at:at + 1], 1.0)
                last.then_inc(vals_clear, 1)

            def mixture(layer):
                def weight_of(b, m):
                    if not isinstance(m, int):
                        return weights[:, b % 2, 1]
                    return weights[:, b % 2, m // HALF_SLABS] if m < EXPERT_SLABS else one[:]

                def add_sum(b):
                    dve.wait_ge(yT_done, NBLK * layer + b + 1)
                    xs = x[:, TPB * b:TPB * (b + 1), :].rearrange("p (k t) d -> p k (t d)", k=2)
                    dve.tensor_tensor(xs, xs, sum_bank(b), ALU.add).then_inc(y_added, 1)

                for b, first in blocks(layer):
                    def step(n, m, s):
                        q = s % 2
                        if isinstance(m, int) and m == 1 and b > 0:
                            add_sum(b - 1)
                        dve.wait_ge(silu_ready, n + 1)
                        if isinstance(m, int) and m == 0:
                            dve.wait_ge(weights_ready, NBLK * layer + b + 1)
                        dve.tensor_tensor(sgc[:, q], sg[:, q], weight_of(b, m), ALU.mult).then_inc(sgc_ready, 1)
                        dve.wait_ge(up_done, n + 1)
                        dve.wait_ge(sgc_ready, n + 1)
                        dve.tensor_tensor(h[:, q], sgc[:, q], bank[2 + q], ALU.mult).then_inc(h_ready, 1)
                        dve.wait_ge(h_hi_ready, n + 1)
                        at_least(dve, down_done, n - 1)
                        dve.tensor_tensor(h_lo[:, q], h[:, q], h_hi[:, q].bitcast(F32), ALU.subtract) \
                           .then_inc(h_lo_ready, 1)
                        if preparation(layer, b, m):
                            prepare(*preparation(layer, b, m), m)
                        if isinstance(m, int) and 0 <= m - STATS_FROM < TPB and b + 2 < NBLK:
                            tile_stats(2 * layer + 1, TPB * (b + 2) + m - STATS_FROM)
                        if layer == 0 and isinstance(m, int) and 6 <= m < 6 + PIECES:
                            clear_values(PIECES * b + m - 6)

                    over_steps(dve, layer, first, step)
                if layer == 0:
                    norm_stats(2, 0)
                    for t in range(2):
                        normalise(2, t)
                add_sum(NBLK - 1)
                dve.wait_ge(y_added, NBLK * (layer + 1))

            mixture(0)

            def heads(t):
                return probs[:, t % 2].rearrange("p (h k) -> p h k", h=HEADS)

            for i in range(NT + 2):
                if i >= 2:
                    j = i - 2
                    dve.wait_ge(pT_done, j + 1)
                    at_least(dve, pv_done, j - 1)
                    dve.tensor_copy(probsT[:, j % 2, BLK:2 * BLK], bank[3]).then_inc(pT_dve, 1)
                if i < NT:
                    if i % TPB == 0 and i // TPB + 1 < NBLK:
                        norm_stats(2, i // TPB + 1)
                    if i + 2 < NT:
                        normalise(2, i + 2)
                    dve.wait_ge(s_done, i + 1)
                    at_least(dve, pT_done, i - 1)
                    for g in range(DK):
                        dst = probs[:, i % 2].rearrange("p (g j n) -> p g j n", g=DK, j=4)[:, g]
                        src = psum[:, 4:8, g * 2 * S:(g + 1) * 2 * S]
                        fl = floor[:, 0:2 * S].unsqueeze(1).broadcast_to([P, 4, 2 * S])
                        last = dve.scalar_tensor_tensor(out=dst, in0=src, scalar=HD ** -0.5, in1=fl,
                                                        op0=ALU.mult, op1=ALU.max)
                    last.then_inc(s_evac, 1)
                    dve.wait_ge(s_evac, i + 1)
                    dve.tensor_reduce(smax[:, i % 2], heads(i), AX, ALU.max).then_inc(smax_ready, 1)
                if i >= 2:
                    j = i - 2
                    dve.wait_ge(pv_done, j + 1)
                    o = bank[1][:, 0:PAIRS * VW].rearrange("p (h w) -> p h w", w=HD + 1)
                    chain(dve.reciprocal(orec[:, j % 2], o[:, :, HD]))
                    chain(dve.tensor_tensor(onorm[:, j % 2].rearrange("p (h d) -> p h d", d=HD), o[:, :, 0:HD],
                                            orec[:, j % 2].unsqueeze(2).broadcast_to([P, HEADS, HD]), ALU.mult))
                    dve.tensor_tensor(x[:, j, :], x[:, j, :], onorm[:, j % 2], ALU.add).then_inc(att_added, 1)
                if PREP_FROM[1] - TPB <= i < PREP_FROM[1] + TPB:
                    dve.wait_ge(att_added, i - 2)
                    tile_stats(3, i - (PREP_FROM[1] - TPB))
                if PREP_FROM[1] <= i:
                    prepare(3, 0, i - PREP_FROM[1])
            dve.wait_ge(att_added, NT)
            mixture(1)

        @block.tensor
        def _(pe):
            def transposes(ln, t):
                pe.wait_ge(xn_ready[ln], t + 1)
                if ln % 2 == 1 and t % TPB == 0:
                    at_least(pe, weights_ready, NBLK * (ln // 2) + t // TPB)
                at_least(pe, tr_evac[ln], t if ln else t - 1)
                for k in range(DK):
                    last = pe.transpose(tr_bank(ln, t)[:, P * k:P * (k + 1)],
                                        xn[:, ln % 2, t % 2, P * k:P * (k + 1)], ident[:])
                last.then_inc(tr_done[ln], 1)

            def three(out, a, b, start, stop):
                pe.matmul(out, a[0], b[0], start=start, stop=False)
                pe.matmul(out, a[0], b[1], start=False, stop=False)
                return pe.matmul(out, a[1], b[0], start=False, stop=stop)

            def logits(ln, t):
                layer, j, i = ln // 2, t // TPB, t % TPB
                pe.wait_ge(tr_evac[ln], t + 1)
                tile = slice(P * i, P * (i + 1))
                for k in range(DK):
                    e = slice((layer * DK + k) * E, (layer * DK + k + 1) * E)
                    last = three(logits_at(ln, j)[:, i, :], (x_hi[:, j % 2, k, tile], x_lo[:, j % 2, k, tile]),
                                 (router_hi[:, e], router_lo[:, e]), k == 0, k == DK - 1)
                if i == TPB - 1:
                    last.then_inc(logits_done, 1)

            def combine_weights(ln, j):
                pe.wait_ge(cwp_ready, NBLK * (ln // 2) + j + 1)
                for t in range(TPB):
                    last = pe.transpose(cwT_at(ln, j)[:, P * t:P * (t + 1)], cwp[:, t, :], identb[:])
                last.then_inc(cwT_done, 1)

            def spread_weights(ln, j):
                pe.wait_ge(cwT_evac, NBLK * (ln // 2) + j + 1)
                for g in range(E // HALF):
                    last = pe.matmul(bank[4 + g], sel[:, g, :], cwT[:], start=True, stop=True)
                last.then_inc(weights_done, 1)

            def prepare(ln, j, m):
                if 2 <= m < 2 + TPB:
                    logits(ln, TPB * j + m - 2)
                if 1 <= m < 1 + TPB:
                    transposes(ln, TPB * j + m - 1)
                if m == 11:
                    combine_weights(ln, j)
                if m == 12:
                    spread_weights(ln, j)

            def prepare_rest(ln, begin):
                for m in range(begin, PREP_STEPS):
                    prepare(ln, 0, m)

            pe.wait_ge(ident_in, 16)
            for t in range(NT):
                transposes(0, t)
            pe.wait_ge(attw_in, 16 * 7)
            pe.wait_ge(ctx_in, 16)
            pe.wait_ge(tr_evac[0], NT)
            for n in range(RH * NBLK):
                hd, cols = n // NBLK, slice(BLK * (n % NBLK), BLK * (n % NBLK + 1))
                at_least(pe, q_evac, n - 1)
                pe.matmul(bank[2 + n % 2], wh[:, hd, :], xT[:, hd, cols], start=True, stop=True).then_inc(q_done, 1)
                at_least(pe, k_evac, n - 1)
                pe.matmul(bank[4 + n % 2], wh[:, hd, :], ctxT[:, hd, cols], start=True, stop=True).then_inc(k_done, 1)
            pe.wait_ge(q_evac, RH * NBLK)
            pe.wait_ge(k_evac, RH * NBLK)
            for hd in range(RH):
                for b in range(B):
                    seq = slice(S * b, S * (b + 1))
                    last = pe.matmul(bank[6][0:S, S * hd:S * (hd + 1)], kT[:, hd, seq], qT[:, hd, seq],
                                     start=b == 0, stop=b == B - 1)
            last.then_inc(ret_scores, 1)
            pe.wait_ge(ret_attn, 1)
            pe.matmul(bank[7][:, 0:RH * S], dup, attn, start=True, stop=True).then_inc(ret_dup, 1)
            for i in range(NT + 4):
                if 1 <= i <= NT:
                    p = (i - 1) % 2
                    pe.wait_ge(v_evac, i)
                    pe.wait_ge(ret_diag, 1)
                    at_least(pe, wy_ready, i - 2)
                    for hd in range(RH):
                        last = pe.matmul(bank[p][:, P * hd:P * (hd + 1)], attn_diag[:, hd, :],
                                         vt[:, p, P * hd:P * (hd + 1)], start=True, stop=True)
                    last.then_inc(o_done, 1)
                if i < NT:
                    p, tile = i % 2, slice(P * i, P * (i + 1))
                    for hd in range(RH):
                        last = pe.matmul(bank[3][:, P * hd:P * (hd + 1)], ctxT[:, hd, tile], wh[:, hd, :],
                                         start=True, stop=True)
                    last.then_inc(v_done, 1)
                    at_least(pe, g_relu, i)
                    for k in range(DK):
                        last = pe.matmul(bank[2][:, 0:D], xT[:, k, tile], wg[:, k, :], start=k == 0,
                                         stop=k == DK - 1)
                    last.then_inc(g_done, 1)
                if 3 <= i < NT + 3:
                    p = (i - 3) % 2
                    pe.wait_ge(wy_ready, i - 2)
                    at_least(pe, wyT_evac, i - 3)
                    for k in range(DK):
                        last = pe.transpose(bank[4][:, P * k:P * (k + 1)], wy[:, p, P * k:P * (k + 1)], ident[:])
                    last.then_inc(wyT_done, 1)
                if 4 <= i:
                    p = (i - 4) % 2
                    pe.wait_ge(wyT_evac, i - 3)
                    at_least(pe, x_added, i - 5)
                    for k in range(DK):
                        last = pe.matmul(bank[6 + p][:, 0:D], wyT[:, p, P * k:P * (k + 1)], wo[:, k, :],
                                         start=k == 0, stop=k == DK - 1)
                    last.then_inc(proj_done, 1)
                if PREP_FROM[0] < i:
                    prepare(1, 0, i - PREP_FROM[0] - 1)

            def mixture(layer):
                def sum_transposed(b):
                    pe.wait_ge(y_evac, NBLK * layer + b + 1)
                    for t in range(TPB):
                        for k in range(DK):
                            at = D * (t % 2) + P * k
                            last = pe.transpose(sum_bank(b)[:, t // 2, at:at + P], ysb[:, k, P * t:P * (t + 1)], ident[:])
                    last.then_inc(yT_done, 1)

                for b, first in blocks(layer):
                    def up(n, m, s):
                        q, r = s % 2, s % RAW
                        pe.wait_ge(up_split, n + 1)

                        def half(out, base):
                            for k in range(DK):
                                w = slice(base + P * k, base + P * (k + 1))
                                last = three(out, (w_hi[:, q, w], w_lo[:, q, w]),
                                             (x_hi[:, b % 2, k], x_lo[:, b % 2, k]), k == 0, k == DK - 1)
                            return last

                        at_least(pe, silu_ready, n - 1)
                        half(bank[q], 0).then_inc(gate_done, 1)
                        if isinstance(m, int) and m == 1 and b > 0:
                            sum_transposed(b - 1)
                        at_least(pe, h_ready, n - 1)
                        half(bank[2 + q], DK * P).then_inc(up_done, 1)

                    def down(n, s, start, stop):
                        q = s % 2
                        pe.wait_ge(down_split, n + 1)
                        pe.wait_ge(h_lo_ready, n + 1)
                        for k in range(DK):
                            w = slice(2 * DK * P + P * k, 2 * DK * P + P * (k + 1))
                            last = three(bank[6 + k], (w_hi[:, q, w], w_lo[:, q, w]), (h_hi[:, q], h_lo[:, q]),
                                         start, stop)
                        last.then_inc(down_done, 1)

                    def step(n, m, s):
                        up(n, m, s)
                        if preparation(layer, b, m):
                            prepare(*preparation(layer, b, m), m)
                        if isinstance(m, int) and m == 1:
                            at_least(pe, y_added, NBLK * layer + b)
                        if not isinstance(m, int) or m > 0:
                            down(n - 1, s - 1, isinstance(m, int) and m == 1, False)
                        elif b > 0:
                            down(n - 1, s - 1, False, True)

                    over_steps(pe, layer, first, step)
                down(first + NM[layer] - 1, first + NM[layer] - 1, False, True)
                sum_transposed(NBLK - 1)

            prepare_rest(1, PREP_STEPS - 2)
            mixture(0)
            transposes(2, 0)
            for i in range(NT + 2):
                if i < NT:
                    p = i % 2
                    pe.wait_ge(keys_ready, 4 * NBLK)
                    pe.wait_ge(tr_evac[2], i + 1)
                    at_least(pe, s_evac, i)
                    for j in range(4):
                        pe.matmul(bank[4 + j][:, 0:4 * S], identb[:], cbig[:], start=True, stop=False,
                                  skip_group_check=True)
                    for b in range(2):
                        for g in range(DK):
                            for j in range(4):
                                rows, q = slice(32 * j, 32 * (j + 1)), slice(S * b, S * (b + 1))
                                seq = slice(S * (2 * i + b), S * (2 * i + b + 1))
                                last = pe.matmul(bank[4 + j][q, 2 * S * g:2 * S * (g + 1)], q_t[rows, p, g, q],
                                                 keys[rows, g, :, seq], start=False, stop=True,
                                                 skip_group_check=True)
                    last.then_inc(s_done, 1)
                at_least(pe, tr_evac[3], min(i - PREP_FROM[1] - 1, TPB))
                if i + 1 < NT:
                    transposes(2, i + 1)
                if i >= 2:
                    j = i - 2
                    p = j % 2
                    pe.wait_ge(vals_ready, 2 * PIECES * NBLK)
                    pe.wait_ge(pT_act, j + 1)
                    pe.wait_ge(pT_dve, j + 1)
                    at_least(pe, att_added, j)
                    if i > PREP_FROM[1] + 5:
                        pe.wait_ge(z_ready, NBLK + 1)
                    for b in range(2):
                        for n in range(PAIRS):
                            q = slice(P * n + S * b, P * n + S * (b + 1))
                            last = pe.matmul(bank[1][S * b:S * (b + 1), VW * n:VW * (n + 1)], probsT[:, p, q],
                                             vals[:, 2 * j + b, n, :], start=True, stop=True)
                    last.then_inc(pv_done, 1)
                if 1 <= i <= NT:
                    j = i - 1
                    p = j % 2
                    pe.wait_ge(probs_ready, j + 1)
                    at_least(pe, pT_act, j)
                    at_least(pe, pT_dve, j)
                    for n in range(PAIRS):
                        last = pe.transpose(bank[2 + n // 4][:, P * (n % 4):P * (n % 4 + 1)],
                                            probs[:, p, P * n:P * (n + 1)], ident[:])
                    last.then_inc(pT_done, 1)
                if PREP_FROM[1] <= i:
                    pe.wait_ge(tr_evac[2], min(i + 2, NT))
                    pe.wait_ge(att_added, i - 1)
                    prepare(3, 0, i - PREP_FROM[1])
            prepare_rest(3, PREP_STEPS - 2)
            mixture(1)


def masks():
    f = np.float32
    gam = (1.0 - f(2.0) ** (-5.0 - np.arange(RH, dtype=f))).astype(f)
    at = np.arange(S, dtype=f)
    expo = at[None, :] - at[:, None]
    decay = np.where(expo[None] <= 0, gam[:, None, None] ** expo[None], 0.0).astype(f)
    decay = decay / np.sqrt(decay.sum(axis=-1, dtype=f))[:, None, :] / np.sqrt(f(P))
    dmask = np.ascontiguousarray(decay.transpose(2, 0, 1).reshape(S, RH * S), f)
    eye = np.eye(S, dtype=f)
    chan = np.arange(P)
    par = np.stack([(chan // HD % 2 == a) for a in range(2)], 1).astype(f)
    sel = np.zeros((P, E // HALF, P), f)
    for k in range(3):
        for g in range(E // HALF):
            sel[E * k + HALF * g + chan // ROWS, g, chan] = 1.0
    masked = np.arange(S)[None, :] > np.arange(S)[:, None]
    masked = np.tile(masked, (2, 4))
    return {
        "identf": np.eye(P, dtype=f), "identb": np.eye(P, dtype=f), "dmask": dmask, "dup": np.hstack([eye, eye]),
        "par": par, "sel": sel, "cbig": np.where(masked, f(-2.0 ** 100), f(0.0)).astype(f),
        "floor": np.where(masked, f(MASKED), f(-3.4e38)).astype(f),
    }


def by_slab(w):
    return w.reshape(E // HALF, HALF, HALF_SLABS, ROWS, D).transpose(0, 2, 1, 3, 4).reshape(E * HID, D)


def slabs(gate, up, down):
    n = gate.shape[0] // P
    parts = [w.reshape(n, P, DK, P).transpose(0, 3, 2, 1).reshape(n, P, DK * P) for w in (gate, up)]
    return np.ascontiguousarray(np.concatenate(parts + [down.reshape(n, P, D)], 2))


def kernel(**inputs):
    import concourse.bacc as bacc
    import ml_dtypes
    from concourse.bass_utils import run_bass_kernel_spmd

    a = {k: np.asarray(v) for k, v in inputs.items()}
    c = masks()
    for k in ("identb", "sel", "cbig"):
        c[k] = c[k].astype(ml_dtypes.bfloat16)
    ctx = a["ctx_2048"]
    pad = np.zeros((NM[1] * P - E * HID - SHARED, D), np.float32)
    up1, sh1 = a["L1_ffn_expert_up_w"], a["L1_ffn_shared_up_w"]
    arrays = {
        "x": a["x"].reshape(TOK, D),
        "ctxT": ctx.reshape(TOK, DK, P).transpose(2, 1, 0),
        "ctxV": ctx.reshape(B, S, PAIRS, 2, HD).transpose(3, 1, 0, 2, 4).reshape(P, DK * TOK),
        "wh": a["L0_xattn_Wh"].transpose(1, 0, 2),
        "wg": a["L0_xattn_wg_w"].reshape(DK, P, D).transpose(1, 0, 2),
        "wo": a["L0_xattn_wo_w"].reshape(DK, P, D).transpose(1, 0, 2),
        "gamma": np.broadcast_to(a["L0_xattn_gn_gamma"], (P, D)),
        "beta": np.broadcast_to(a["L0_xattn_gn_beta"], (P, D)),
        "router": np.stack([a["L0_ffn_gate_w"], a["L1_ffn_gate_w"]]).reshape(2, E, DK, P).transpose(3, 0, 2, 1)
                    .reshape(P, 2 * DK * E),
        "w0": slabs(by_slab(a["L0_ffn_w_gate"]), by_slab(a["L0_ffn_w_up"]),
                    by_slab(a["L0_ffn_w_down"].transpose(0, 2, 1))),
        "w1": slabs(np.concatenate([by_slab(up1[:, :HID]), sh1[:SHARED], pad]),
                    np.concatenate([by_slab(up1[:, HID:]), sh1[SHARED:], pad]),
                    np.concatenate([by_slab(a["L1_ffn_expert_down_w"].transpose(0, 2, 1)),
                                    a["L1_ffn_shared_down_w"].T, pad])),
        "sel": c["sel"], "identf": c["identf"], "identb": c["identb"], "dmask": c["dmask"], "dup": c["dup"],
        "par": c["par"], "cbig": c["cbig"], "floor": c["floor"],
    }
    arrays = {f"in_{k}": np.ascontiguousarray(v) for k, v in arrays.items()}
    nc = bacc.Bacc("TRN2", target_bir_lowering=False, num_devices=1)
    aps = [nc.dram_tensor(k, v.shape, mybir.dt.from_np(v.dtype), kind="ExternalInput").ap()
           for k, v in arrays.items()]
    out = nc.dram_tensor("out", (TOK, D), F32, kind="ExternalOutput").ap()
    retention_mixture_layers(nc, *aps, out)
    got = run_bass_kernel_spmd(nc, [arrays], core_ids=[0])
    return got.results[0]["out"].reshape(B, S, D)
```

```python
from contextlib import ExitStack

import numpy as np

import concourse.bass as bass
from concourse import mybir

F32 = mybir.dt.float32
F32R = mybir.dt.float32r
BF16 = mybir.dt.bfloat16
ALU = mybir.AluOpType
ACT = mybir.ActivationFunctionType
AX = mybir.AxisListType.X

P = 128
B, S, D = 32, 64, 256
TOK = B * S
NT = TOK // P
DK = D // P
BLK = 512
NBLK = TOK // BLK
TPB = BLK // P
E = 16
HID = 176
SHARED = 352
EXPERT_SLABS = E * HID // P
NM = (EXPERT_SLABS, -(-(E * HID + SHARED) // P))
ROWS = 16
HALF = P // ROWS
HALF_SLABS = HID // ROWS
TOPK = (6, 4)
GROUPS, TOPG = 4, 2
HEADS, HD = 16, 16
RH = 2
PAIRS = HEADS // 2
HPH = HEADS // DK
SPREAD_ACT = 4
VW = 2 * (HD + 1)
WCOLS = 3 * DK * P
LN_EPS, GN_EPS = 1e-5, 1e-3
MASKED = -10000.0
RAW, UNROLL = 4, 4
PREP_STEPS = 13
STATS_FROM = 9
PREP_FROM = (7, 6)
PIECES = 2


def retention_mixture_layers(nc, x_d, ctxT_d, ctxV_d, wh_d, wg_d, wo_d, gamma_d, beta_d, router_d,
                             w0_d, w1_d, sel_d, identf_d, identb_d, dmask_d, dup_d, head_mask_d,
                             cbig_d, floor_d, out_d):
    w_d = (w0_d, w1_d)
    with ExitStack() as ctx:
        def sb(name, shape, dt=F32):
            return ctx.enter_context(nc.sbuf_tensor(name, shape, dt))

        def sem(name):
            return ctx.enter_context(nc.semaphore(name))

        x = sb("x", [P, NT, D])
        ident = sb("ident", [P, P])
        identb = sb("identb", [P, P], BF16)
        mean_var = sb("mean_var", [P, 4, NT, 2])
        var_eps = sb("var_eps", [P, 4, NT])
        rstd = sb("rstd", [P, 4, NT])
        minus_half = sb("minus_half", [P, NT])
        stats = sb("stats", [P, NT, 6])
        xn = sb("xn", [P, 2, 2, D])
        x_hi = sb("x_hi", [P, 2, DK, BLK], F32R)
        x_lo = sb("x_lo", [P, 2, DK, BLK], F32R)
        big = sb("big", [P, 4 * TOK])
        xT = big[:, 0:DK * TOK].rearrange("p (k n) -> p k n", k=DK)
        qT = big[:, DK * TOK:2 * DK * TOK].rearrange("p (k n) -> p k n", k=DK)
        keys = big[:, 0:2 * DK * HPH * P].rearrange("p (t g b h s) -> p t g b h s", t=2, g=DK, b=2, h=HPH)
        ctxT = sb("ctxT", [P, DK, TOK])
        ctxV = sb("ctxV", [P, B, PAIRS, HD])
        val_buf = sb("val_buf", [P, B * PAIRS * VW])
        kT = val_buf[:, 0:DK * TOK].rearrange("p (k n) -> p k n", k=DK)
        vals = val_buf[:, :].rearrange("p (b i w) -> p b i w", b=B, i=PAIRS)
        work = sb("work", [P, 8 * BLK])

        def pair_of(at, width):
            return work[:, at:at + 2 * width].rearrange("p (s n) -> p s n", s=2)

        vt, gate, gate_g, gate_b, yn, wy, wyT = (pair_of(2 * D * n, D) for n in range(7))
        sg, sgc, h = (pair_of(2 * BLK * n, BLK) for n in range(3))
        ysb = pair_of(6 * BLK, BLK)
        probs, probsT = (pair_of(4 * BLK * n, 2 * BLK) for n in range(2))
        free_at = [DK * TOK]

        def until_values(width):
            free_at[0] += width
            return val_buf[:, free_at[0] - width:free_at[0]]

        wh = until_values(RH * P).rearrange("p (h n) -> p h n", h=RH)
        wg = until_values(DK * D).rearrange("p (k n) -> p k n", k=DK)
        wo = until_values(DK * D).rearrange("p (k n) -> p k n", k=DK)
        gamma = until_values(D)
        beta = until_values(D)
        dmask = until_values(RH * S)[0:S]
        dup = until_values(P)[0:S]
        decayed = until_values(RH * S)[0:S]
        attn = until_values(RH * S)[0:S]
        attn_diag = until_values(RH * P).rearrange("p (h n) -> p h n", h=RH)
        gn_stats = sb("gn_stats", [P, 2, 6])
        gn_mv = sb("gn_mv", [P, 2, 2])
        gn_ve = sb("gn_ve", [P, 2])
        gn_rstd = sb("gn_rstd", [P, 2])
        head_mask = sb("head_mask", [P, HPH])
        cbig = sb("cbig", [P, BLK], BF16)
        floor = sb("floor", [P, S])
        smax = sb("smax", [P, 2, HEADS])
        orec = sb("orec", [P, 2, HEADS])
        onorm = sb("onorm", [P, 2, D])
        q_t = sb("q_t", [P, 2, DK, P])
        router = sb("router", [P, 2 * DK * E])
        router_parts = sb("router_parts", [P, 2 * DK, 2, E], F32R)
        z = sb("z", [P, TPB, E])
        ez = sb("ez", [P, TPB, E])
        zmax = sb("zmax", [P, TPB])
        zsum = sb("zsum", [P, TPB])
        zrec = sb("zrec", [P, TPB])
        cand = sb("cand", [P, TPB, E + 4])
        left = sb("left", [P, TPB, E + 4])
        top = sb("top", [P, TPB, 8])
        gcand = sb("gcand", [P, TPB, GROUPS + 8 - TOPG])
        gleft = sb("gleft", [P, TPB, GROUPS + 8 - TOPG])
        gmask = sb("gmask", [P, TPB, GROUPS])
        cw = sb("cw", [P, TPB, E])
        cwp = sb("cwp", [P, TPB, P], BF16)
        cwT = sb("cwT", [P, BLK], BF16)
        weights = sb("weights", [P, 2, E // HALF, BLK])
        one = sb("one", [P, BLK])
        w_raw = sb("w_raw", [P, RAW, WCOLS])
        sel = sb("sel", [P, E // HALF, P], BF16)
        w_hi = sb("w_hi", [P, 2, WCOLS], F32R)
        w_lo = sb("w_lo", [P, 2, WCOLS], F32R)
        h_hi = sb("h_hi", [P, 2, BLK], F32R)
        h_lo = sb("h_lo", [P, 2, BLK], F32R)

        psum = ctx.enter_context(nc.psum_tensor("psum", [P, 8, 512], F32))
        bank = [psum[:, i, :] for i in range(8)]
        prep_bank = bank[5]

        def xn_of(ln, t):
            return xn[:, t // 2 % 2 if ln == 0 else ln % 2, t % 2]

        def tr_bank(ln, t):
            if ln == 0:
                return bank[t % 4][:, 0:D]
            if ln == 2:
                return bank[0][:, 0:D]
            return bank[0][:, D:2 * D] if (ln, t // TPB) == (3, 0) else prep_bank[:, 0:D]

        def sum_bank(b):
            return psum[:, 6:8, :] if b + 1 < NBLK else psum[:, 2:4, :]

        def logits_at(ln, j):
            at = bank[1] if (ln, j) == (3, 0) else prep_bank
            return at[:, PAIRS * VW:PAIRS * VW + TPB * 2 * E].rearrange("p (t k e) -> p t k e", t=TPB, k=2)

        def cwT_at(ln, j):
            if (ln, j) == (3, 0):
                return bank[0].bitcast(BF16)[:, BLK:2 * BLK]
            return prep_bank.bitcast(BF16)[:, 0:BLK]

        x_in = [sem(f"x_in{j}") for j in range(NBLK)]
        ctx_in = [sem(f"ctx_in{j}") for j in range(NBLK)]
        ident_in, consts_in, wh_in, attw_in, vals_in = (
            sem(n) for n in ("ident_in", "consts_in", "wh_in", "attw_in", "vals_in"))
        var_ready, rstd_ready, xn_ready, tr_done, tr_evac = (
            [sem(f"{n}{ln}") for ln in range(4)]
            for n in ("var_ready", "rstd_ready", "xn_ready", "tr_done", "tr_evac"))
        memset_done, tr_hi = sem("memset_done"), sem("tr_hi")
        q_done, k_done, q_evac, k_evac, ret_scores, ret_attn, ret_dup, ret_diag = (
            sem(n) for n in ("q_done", "k_done", "q_evac", "k_evac", "ret_scores", "ret_attn", "ret_dup", "ret_diag"))
        v_done, v_evac, g_done, g_relu, gates_ready, o_done, gn_var, gn_ready, wy_ready, wyT_done, wyT_evac, \
            proj_done, x_added = (sem(n) for n in (
                "v_done", "v_evac", "g_done", "g_relu", "gates_ready", "o_done", "gn_var", "gn_ready", "wy_ready",
                "wyT_done", "wyT_evac", "proj_done", "x_added"))
        router_split, logits_done, z_ready, ez_ready, cwp_ready, cwT_done, cwT_evac, weights_done, weights_ready = (
            sem(n) for n in ("router_split", "logits_done", "z_ready", "ez_ready", "cwp_ready", "cwT_done", "cwT_evac",
                             "weights_done", "weights_ready"))
        w_in = [sem(f"w_in{j}") for j in range(RAW)]
        up_hi, down_hi, up_split, down_split, gate_done, up_done, down_done = (
            sem(n) for n in ("up_hi", "down_hi", "up_split", "down_split", "gate_done", "up_done", "down_done"))
        silu_ready, sgc_ready, h_ready, h_hi_ready, h_lo_ready, y_evac, yT_done, y_added = (
            sem(n) for n in ("silu_ready", "sgc_ready", "h_ready", "h_hi_ready", "h_lo_ready", "y_evac",
                             "yT_done", "y_added"))
        keys_act, keys_pool, vals_clear, vals_ready, s_done, s_evac, smax_ready, shifted, probs_ready, pT_done, \
            pT_evac, pv_done, att_added = (sem(n) for n in (
                "keys_act", "keys_pool", "vals_clear", "vals_ready", "s_done", "s_evac", "smax_ready", "shifted",
                "probs_ready", "pT_done", "pT_evac", "pv_done", "att_added"))
        dve_chain, pool_chain, out_done = sem("dve_chain"), sem("pool_chain"), sem("out_done")

        STEPS = NBLK * sum(NM)

        def blocks(layer):
            return [(b, layer * NBLK * NM[0] + b * NM[layer]) for b in range(NBLK)]

        def over_steps(eng, layer, first, step):
            turns = (EXPERT_SLABS - PREP_STEPS - 1) // UNROLL
            peel = EXPERT_SLABS - 1 - turns * UNROLL
            for m in range(peel):
                step(first + m, m, first + m)
            with eng.Fori(0, turns) as turn:
                for u in range(UNROLL):
                    m = turn * UNROLL + (peel + u)
                    step(m + first, m, first + peel + u)
            for m in range(EXPERT_SLABS - 1, NM[layer]):
                step(first + m, m, first + m)

        def piece_of(k):
            n = B // (PIECES * NBLK)
            return slice(n * k, n * (k + 1))

        def keys_of(t, head):
            return keys[:, t % 2, :, :, head], ctxT[:, :, P * t:P * (t + 1)].rearrange("p g (b s) -> p g b s", b=2)

        def preparation(layer, b, m):
            return (2 * layer + 1, b + 1) if isinstance(m, int) and m < PREP_STEPS and b + 1 < NBLK else None

        def at_least(eng, semaphore, value):
            if not isinstance(value, int) or value > 0:
                eng.wait_ge(semaphore, value)

        block = ctx.enter_context(nc.Block())

        @block.sync
        def _(sp):
            sp.dma_start(ident[:], identf_d).then_inc(ident_in, 16)
            for j in range(NBLK):
                sp.dma_start(x[:, TPB * j:TPB * (j + 1), :],
                             x_d[BLK * j:BLK * (j + 1), :].rearrange("(t p) d -> p t d", p=P)).then_inc(x_in[j], 16)
                if j == 0:
                    sp.dma_start(wh, wh_d).then_inc(wh_in, 16)
                cols = slice(BLK * j, BLK * (j + 1))
                sp.dma_start(ctxT[:, :, cols], ctxT_d[:, :, cols]).then_inc(ctx_in[j], 16)
            for dst, src in ((wg, wg_d), (wo, wo_d), (gamma, gamma_d), (beta, beta_d),
                             (dmask, dmask_d), (dup, dup_d)):
                sp.dma_start(dst, src).then_inc(attw_in, 16)
            for dst, src in ((identb[:], identb_d), (sel[:], sel_d), (router[:], router_d),
                             (head_mask[:], head_mask_d), (cbig[:], cbig_d), (floor[:], floor_d)):
                sp.dma_start(dst, src).then_inc(consts_in, 16)
            sp.dma_start(ctxV[:].rearrange("p b i d -> p (b i d)"), ctxV_d).then_inc(vals_in, 16)

            def store(b):
                sp.wait_ge(y_added, NBLK + b + 1)
                sp.dma_start(out_d[BLK * b:BLK * (b + 1), :].rearrange("(t p) d -> p t d", p=P),
                             x[:, TPB * b:TPB * (b + 1), :]).then_inc(out_done, 16)

            def load(n, m, s):
                at_least(sp, down_split, n - (RAW - 1))
                sp.dma_start(w_raw[:, s % RAW, :], w_of[m]).then_inc(w_in[s % RAW], 16)

            for layer in range(2):
                w_of = w_d[layer]
                for b, first in blocks(layer):
                    over_steps(sp, layer, first, load)
                    if layer == 1 and b > 0:
                        store(b - 1)
            store(NBLK - 1)
            sp.wait_ge(out_done, 16 * NBLK)

        @block.gpsimd
        def _(pool):
            count = [0]

            def chain(ins):
                count[0] += 1
                ins.then_inc(pool_chain, 1)
                pool.wait_ge(pool_chain, count[0])

            def norm_scale(ln, j):
                t = slice(TPB * j, TPB * (j + 1))
                pool.wait_ge(var_ready[ln], j + 1)
                chain(pool.tensor_scalar(var_eps[:, ln, t], mean_var[:, ln, t, 1], LN_EPS, None, ALU.add))
                pool.tensor_tensor(rstd[:, ln, t], var_eps[:, ln, t], minus_half[:, t], ALU.pow).then_inc(rstd_ready[ln], 1)

            chain(pool.memset(minus_half[:], -0.5))
            pool.memset(attn_diag, 0.0).then_inc(memset_done, 1)
            for k in range(8 - TOPK[1]):
                pool.memset(cand[:, :, E + k:E + k + 1], 2.0 + k).then_inc(memset_done, 1)
            for k in range(8 - TOPG):
                pool.memset(gcand[:, :, GROUPS + k:GROUPS + k + 1], 2.0 + k).then_inc(memset_done, 1)
            pool.memset(cwp[:], 0.0).then_inc(memset_done, 1)
            pool.memset(one[:], 1.0).then_inc(memset_done, 1)
            for j in range(NBLK):
                norm_scale(0, j)
            pool.wait_ge(attw_in, 16 * 6)
            for t in range(NT):
                p = t % 2
                if t in (PREP_FROM[0], PREP_FROM[0] + TPB):
                    norm_scale(1, (t - PREP_FROM[0]) // TPB)
                pool.wait_ge(g_relu, t + 1)
                at_least(pool, wy_ready, t - 1)
                pool.tensor_tensor(gate_g[:, p], gate[:, p], gamma, ALU.mult)
                pool.tensor_tensor(gate_b[:, p], gate[:, p], beta, ALU.mult).then_inc(gates_ready, 1)
                pool.wait_ge(gn_var, t + 1)
                chain(pool.tensor_scalar(gn_ve[:, p:p + 1], gn_mv[:, p, 1:2], GN_EPS, None, ALU.add))
                pool.tensor_tensor(gn_rstd[:, p:p + 1], gn_ve[:, p:p + 1], minus_half[:, 0:1],
                                   ALU.pow).then_inc(gn_ready, 1)

            def split_up(n, s):
                q, r, up = s % 2, s % RAW, slice(0, 2 * DK * P)
                pool.wait_ge(up_hi, n + 1)
                pool.tensor_tensor(w_lo[:, q, up], w_raw[:, r, up], w_hi[:, q, up], ALU.subtract) \
                    .then_inc(up_split, 1)

            def split_down(n, s):
                q, r, down = s % 2, s % RAW, slice(2 * DK * P, WCOLS)
                pool.wait_ge(down_hi, n + 1)
                pool.tensor_tensor(w_lo[:, q, down], w_raw[:, r, down], w_hi[:, q, down], ALU.subtract) \
                    .then_inc(down_split, 1)

            def values_piece(b, k):
                a, piece = k % 2, PIECES * b + k // 2
                rows, at, seqs = slice(S * a, S * (a + 1)), a * (HD + 1), piece_of(piece)
                pool.wait_ge(vals_clear, piece + 1)
                pool.wait_ge(vals_in, 16)
                pool.tensor_copy(vals[rows, seqs, :, at:at + HD], ctxV[rows, seqs]).then_inc(vals_ready, 1)
                pool.wait_ge(vals_ready, 2 * PIECES * b + k + 1)

            split_up(0, 0)
            for layer in range(2):
                for b, first in blocks(layer):
                    def step(n, m, s):
                        if not (isinstance(n, int) and n == STEPS - 1):
                            split_up(n + 1, s + 1)
                        split_down(n, s)
                        if isinstance(m, int) and m == EXPERT_SLABS - 1 and b + 2 < NBLK:
                            norm_scale(2 * layer + 1, b + 2)
                        if layer == 0 and isinstance(m, int) and 9 <= m < 9 + 2 * PIECES:
                            pool.wait_ge(down_split, n + 1)
                            values_piece(b, m - 9)

                    over_steps(pool, layer, first, step)
                if layer == 0:
                    def spread(t):
                        at_least(pool, s_done, t - 1)
                        for head in range(SPREAD_ACT, HPH):
                            dst, src = keys_of(t, head)
                            mask = head_mask[:, head:head + 1].unsqueeze(2).unsqueeze(3).broadcast_to([P, DK, 2, S])
                            last = pool.tensor_tensor(dst, src, mask, ALU.mult)
                        last.then_inc(keys_pool, 1)

                    spread(0)
                    norm_scale(2, 0)
                    for t in range(NT):
                        if t + 1 < NT:
                            spread(t + 1)
                        if t % TPB == 1 and t // TPB + 1 < NBLK:
                            norm_scale(2, t // TPB + 1)
                        if t in (PREP_FROM[1], PREP_FROM[1] + TPB):
                            norm_scale(3, (t - PREP_FROM[1]) // TPB)
                        pool.wait_ge(smax_ready, t + 1)
                        sc = probs[:, t % 2].rearrange("p (h k) -> p h k", h=HEADS)
                        mx = smax[:, t % 2].unsqueeze(2).broadcast_to([P, HEADS, S])
                        pool.tensor_tensor(sc, sc, mx, ALU.subtract).then_inc(shifted, 1)

        @block.scalar
        def _(act):
            def high(ln, t):
                act.wait_ge(tr_done[ln], t + 1)
                cols = slice(P * (t % TPB), P * (t % TPB + 1))
                act.copy(x_hi[:, t // TPB % 2, :, cols],
                         tr_bank(ln, t).rearrange("p (k n) -> p k n", k=DK)).then_inc(tr_hi, 1)

            def router_exp(ln, j):
                act.wait_ge(z_ready, NBLK * (ln // 2) + j + 1)
                act.activation(ez[:], z[:], ACT.Exp).then_inc(ez_ready, 1)

            def combine_weights(ln, j):
                act.wait_ge(cwT_done, NBLK * (ln // 2) + j + 1)
                at_least(act, weights_done, NBLK * (ln // 2) + j)
                act.copy(cwT[:], cwT_at(ln, j)).then_inc(cwT_evac, 1)

            def spread_weights(ln, j):
                act.wait_ge(weights_done, NBLK * (ln // 2) + j + 1)
                act.copy(weights[:, j % 2], psum[:, 4:6, :]).then_inc(weights_ready, 1)

            def prepare(ln, j, m):
                if 1 <= m < 1 + TPB:
                    high(ln, TPB * j + m - 1)
                if m == 5:
                    router_exp(ln, j)
                if m == 11:
                    combine_weights(ln, j)
                if m == 12:
                    spread_weights(ln, j)

            def prepare_rest(ln, begin):
                for m in range(begin, PREP_STEPS):
                    prepare(ln, 0, m)

            def up_high(n, s):
                q, r, up = s % 2, s % RAW, slice(0, 2 * DK * P)
                act.wait_ge(w_in[r], (n - r) * (16 // RAW) + 16)
                at_least(act, up_done, n - 1)
                act.copy(w_hi[:, q, up], w_raw[:, r, up]).then_inc(up_hi, 1)

            for t in range(NT):
                act.wait_ge(tr_done[0], t + 1)
                act.copy(xT[:, :, P * t:P * (t + 1)],
                         tr_bank(0, t).rearrange("p (k n) -> p k n", k=DK)).then_inc(tr_evac[0], 1)
                if t % TPB == TPB - 1:
                    for n in range(RH * (t // TPB), RH * (t // TPB + 1)):
                        act.wait_ge(k_done, n + 1)
                        act.copy(kT[:, n % RH, BLK * (n // RH):BLK * (n // RH + 1)], bank[4 + n % 2]).then_inc(k_evac, 1)
            for i in range(NT + 3):
                if i < NT:
                    act.wait_ge(v_done, i + 1)
                    at_least(act, o_done, i - 1)
                    act.copy(vt[:, i % 2], bank[3][:, 0:D]).then_inc(v_evac, 1)
                    act.wait_ge(g_done, i + 1)
                    at_least(act, gates_ready, i - 1)
                    act.activation(gate[:, i % 2], bank[2][:, 0:D], ACT.Relu).then_inc(g_relu, 1)
                if i >= 3:
                    j = i - 3
                    act.wait_ge(wyT_done, j + 1)
                    at_least(act, proj_done, j - 1)
                    act.copy(wyT[:, j % 2], bank[4][:, 0:D]).then_inc(wyT_evac, 1)
                if PREP_FROM[0] < i:
                    prepare(1, 0, i - PREP_FROM[0] - 1)
                if i == NT // 2:
                    up_high(0, 0)

            def spread(t):
                at_least(act, s_done, t - 1)
                for head in range(SPREAD_ACT):
                    dst, src = keys_of(t, head)
                    last = act.activation(dst, src, ACT.Copy, scale=head_mask[:, head:head + 1])
                last.then_inc(keys_act, 1)

            def mixture(layer):
                def sum_to_sbuf(b, through):
                    act.wait_ge(down_done, through)
                    at_least(act, yT_done, NBLK * layer + b)
                    act.copy(ysb, psum[:, 6:8, :]).then_inc(y_evac, 1)

                for b, first in blocks(layer):
                    def step(n, m, s):
                        q, r, down = s % 2, s % RAW, slice(2 * DK * P, WCOLS)
                        if isinstance(m, int) and m == 1 and b > 0:
                            sum_to_sbuf(b - 1, first)
                        if not (isinstance(n, int) and n == STEPS - 1):
                            up_high(n + 1, s + 1)
                        act.wait_ge(gate_done, n + 1)
                        at_least(act, sgc_ready, n - 1)
                        act.activation(sg[:, q], bank[q], ACT.Silu).then_inc(silu_ready, 1)
                        at_least(act, down_done, n - 1)
                        act.copy(w_hi[:, q, down], w_raw[:, r, down]).then_inc(down_hi, 1)
                        if preparation(layer, b, m) and m != 5:
                            prepare(*preparation(layer, b, m), m)
                        act.wait_ge(h_ready, n + 1)
                        act.copy(h_hi[:, q], h[:, q]).then_inc(h_hi_ready, 1)
                        if preparation(layer, b, m) and m == 5:
                            prepare(*preparation(layer, b, m), m)

                    over_steps(act, layer, first, step)
                if layer == 0:
                    spread(0)
                sum_to_sbuf(NBLK - 1, first + NM[layer])

            prepare_rest(1, PREP_STEPS - 2)
            mixture(0)
            def queries(t):
                act.wait_ge(tr_done[2], t + 1)
                at_least(act, s_done, t - 1)
                act.copy(q_t[:, t % 2], tr_bank(2, t).rearrange("p (k n) -> p k n", k=DK)).then_inc(tr_evac[2], 1)

            queries(0)
            for i in range(NT + 2):
                if i >= 2:
                    j = i - 2
                    act.wait_ge(pT_done, j + 1)
                    at_least(act, pv_done, j - 1)
                    act.copy(probsT[:, j % 2], psum[:, 2:4, :].rearrange("p k n -> p (k n)")).then_inc(pT_evac, 1)
                if i + 1 < NT:
                    spread(i + 1)
                    queries(i + 1)
                if 1 <= i <= NT:
                    act.wait_ge(shifted, i)
                    act.activation(probs[:, (i - 1) % 2], probs[:, (i - 1) % 2], ACT.Exp).then_inc(probs_ready, 1)
                if PREP_FROM[1] <= i:
                    prepare(3, 0, i - PREP_FROM[1])
            prepare_rest(3, PREP_STEPS - 1)
            mixture(1)

        @block.vector
        def _(dve):
            count = [0]

            def chain(ins):
                count[0] += 1
                ins.then_inc(dve_chain, 1)
                dve.wait_ge(dve_chain, count[0])

            def norm_stats(ln, j):
                for t in range(TPB * j, TPB * (j + 1)):
                    last = dve.bn_stats(stats[:, t, :], x[:, t, :])
                chain(last)
                for t in range(TPB * j, TPB * (j + 1)):
                    last = dve.bn_aggr(mean_var[:, ln, t, :], stats[:, t, :])
                last.then_inc(var_ready[ln], 1)

            def tile_stats(ln, t):
                chain(dve.bn_stats(stats[:, t, :], x[:, t, :]))
                last = dve.bn_aggr(mean_var[:, ln, t, :], stats[:, t, :])
                if t % TPB == TPB - 1:
                    last.then_inc(var_ready[ln], 1)

            def normalise(ln, t):
                if t % TPB == 0:
                    dve.wait_ge(rstd_ready[ln], t // TPB + 1)
                at_least(dve, tr_done[ln], t - (1 if ln else 3))
                dve.tensor_scalar(xn_of(ln, t), x[:, t, :], mean_var[:, ln, t, 0:1], rstd[:, ln, t:t + 1],
                                  ALU.subtract, ALU.mult).then_inc(xn_ready[ln], 1)

            def split_routers():
                whole = router[:].rearrange("p (k e) -> p k e", e=E)
                chain(dve.tensor_copy(router_parts[:, :, 0], whole))
                dve.tensor_tensor(router_parts[:, :, 1], whole, router_parts[:, :, 0].bitcast(F32),
                                  ALU.subtract).then_inc(router_split, 1)

            def low(ln, t):
                dve.wait_ge(tr_hi, NT * (ln // 2) + t + 1)
                part, cols = t // TPB % 2, slice(P * (t % TPB), P * (t % TPB + 1))
                dve.tensor_tensor(x_lo[:, part, :, cols], tr_bank(ln, t).rearrange("p (k n) -> p k n", k=DK),
                                  x_hi[:, part, :, cols].bitcast(F32), ALU.subtract).then_inc(tr_evac[ln], 1)

            def over(a, n=E):
                return a.unsqueeze(2).broadcast_to([P, TPB, n])

            def router_shift(ln, j):
                dve.wait_ge(logits_done, NBLK * (ln // 2) + j + 1)
                chain(dve.tensor_copy(z[:], logits_at(ln, j)[:, :, 0]))
                chain(dve.tensor_tensor(z[:], z[:], logits_at(ln, j)[:, :, 1], ALU.add))
                chain(dve.tensor_reduce(zmax[:], z[:], AX, ALU.max))
                dve.tensor_tensor(z[:], z[:], over(zmax[:]), ALU.subtract).then_inc(z_ready, 1)

            scores = cand[:, :, 0:E]

            def router_softmax(ln, j):
                layer = ln // 2
                dve.wait_ge(ez_ready, NBLK * layer + j + 1)
                chain(dve.tensor_reduce(zsum[:], ez[:], AX, ALU.add))
                chain(dve.reciprocal(zrec[:], zsum[:]))
                chain(dve.tensor_tensor(scores, ez[:], over(zrec[:]), ALU.mult))

            def router_groups(ln, j):
                if ln // 2 == 1:
                    chain(dve.tensor_reduce(gcand[:, :, 0:GROUPS],
                                            scores.rearrange("p t (g e) -> p t g e", g=GROUPS), AX, ALU.max))
                    for t in range(TPB):
                        last = dve.max(top[:, t, :], gcand[:, t, :])
                    chain(last)
                    for t in range(TPB):
                        last = dve.match_replace(gleft[:, t, :], top[:, t, :], gcand[:, t, :], -1.0)
                    chain(last)
                    chain(dve.tensor_scalar(gmask[:], gleft[:, :, 0:GROUPS], 0.0, None, ALU.is_lt))
                    for g in range(GROUPS):
                        e = slice(g * E // GROUPS, (g + 1) * E // GROUPS)
                        last = dve.tensor_tensor(scores[:, :, e], scores[:, :, e],
                                                 over(gmask[:, :, g], E // GROUPS), ALU.mult)
                    chain(last)

            def router_choose(ln, j):
                layer = ln // 2
                width = E + 8 - TOPK[layer]
                for t in range(TPB):
                    last = dve.max(top[:, t, :], cand[:, t, 0:width])
                chain(last)
                for t in range(TPB):
                    last = dve.match_replace(left[:, t, 0:width], top[:, t, :], cand[:, t, 0:width], 0.0)
                chain(last)
                chain(dve.tensor_tensor(cw[:], scores, left[:, :, 0:E], ALU.subtract))

            def router_norm(ln, j):
                if ln // 2 == 1:
                    chain(dve.tensor_reduce(zsum[:], cw[:], AX, ALU.add))
                    chain(dve.tensor_scalar(zsum[:], zsum[:], 1e-20, None, ALU.add))
                    chain(dve.reciprocal(zrec[:], zsum[:]))
                    chain(dve.tensor_tensor(cw[:], cw[:], over(zrec[:]), ALU.mult))

            def weight_parts(ln, j):
                at_least(dve, cwT_done, NBLK * (ln // 2) + j)
                parts = [cwp[:, :, E * k:E * (k + 1)] for k in range(3)]
                chain(dve.tensor_copy(parts[0], cw[:]))
                chain(dve.tensor_tensor(z[:], cw[:], parts[0], ALU.subtract))
                chain(dve.tensor_copy(parts[1], z[:]))
                dve.tensor_tensor(parts[2], z[:], parts[1], ALU.subtract).then_inc(cwp_ready, 1)

            router_stages = (router_softmax, router_groups, router_choose, router_norm, weight_parts)

            def prepare(ln, j, m):
                if 1 <= m < 1 + TPB:
                    low(ln, TPB * j + m - 1)
                if m < TPB:
                    normalise(ln, TPB * j + m)
                if m == 5:
                    router_shift(ln, j)
                for at, stage in enumerate(router_stages):
                    if m == 6 + at:
                        stage(ln, j)

            for j in range(NBLK):
                dve.wait_ge(x_in[j], 16)
                norm_stats(0, j)
                if j != 1:
                    for t in range(TPB * max(j - 1, 0), TPB * max(j, 1)):
                        normalise(0, t)
            for t in range(NT - TPB, NT):
                normalise(0, t)
            for n in range(RH * NBLK):
                hd, j = n // NBLK, n % NBLK
                dve.wait_ge(q_done, n + 1)
                dve.tensor_copy(qT[:, hd, BLK * j:BLK * (j + 1)], bank[2 + n % 2]).then_inc(q_evac, 1)
            dve.wait_ge(consts_in, 16 * 6)
            split_routers()
            dve.wait_ge(memset_done, 13)
            dve.wait_ge(ret_scores, 1)
            dve.wait_ge(attw_in, 16 * 6)
            chain(dve.tensor_tensor(decayed, bank[6][0:S, 0:RH * S], dmask, ALU.mult))
            chain(dve.scalar_tensor_tensor(out=attn, in0=decayed, scalar=-1.0, in1=decayed, op0=ALU.mult, op1=ALU.max))
            dve.tensor_scalar(attn, attn, 1.0, None, ALU.max).then_inc(ret_attn, 1)
            dve.wait_ge(ret_dup, 1)
            for a in range(2):
                rows = slice(S * a, S * (a + 1))
                last = dve.tensor_copy(attn_diag[rows, :, rows],
                                       bank[7][rows, 0:RH * S].rearrange("p (h s) -> p h s", h=RH))
            last.then_inc(ret_diag, 1)
            for i in range(NT + 3):
                if 1 <= i <= NT:
                    j = i - 1
                    p = j % 2
                    dve.wait_ge(gn_ready, j + 1)
                    chain(dve.tensor_scalar(yn[:, p], bank[p][:, 0:D], gn_mv[:, p, 0:1], gn_rstd[:, p:p + 1],
                                            ALU.subtract, ALU.mult))
                    dve.wait_ge(gates_ready, j + 1)
                    at_least(dve, wyT_done, j - 1)
                    chain(dve.tensor_tensor(wy[:, p], yn[:, p], gate_g[:, p], ALU.mult))
                    dve.tensor_tensor(wy[:, p], wy[:, p], gate_b[:, p], ALU.add).then_inc(wy_ready, 1)
                if i < NT:
                    p = i % 2
                    dve.wait_ge(o_done, i + 1)
                    chain(dve.bn_stats(gn_stats[:, p, :], bank[p][:, 0:D]))
                    at_least(dve, gn_ready, i - 1)
                    dve.bn_aggr(gn_mv[:, p, :], gn_stats[:, p, :]).then_inc(gn_var, 1)
                if i >= 3:
                    j = i - 3
                    dve.wait_ge(proj_done, j + 1)
                    dve.tensor_tensor(x[:, j, :], x[:, j, :], bank[6 + j % 2][:, 0:D], ALU.add).then_inc(x_added, 1)
                if PREP_FROM[0] - TPB <= i < PREP_FROM[0] + TPB:
                    tile = i - (PREP_FROM[0] - TPB)
                    dve.wait_ge(x_added, tile + 1)
                    tile_stats(1, tile)
                if PREP_FROM[0] <= i:
                    prepare(1, 0, i - PREP_FROM[0])

            def clear_values(piece):
                seqs = piece_of(piece)
                chain(dve.memset(vals[:, seqs], 0.0))
                for a in range(2):
                    rows, at = slice(S * a, S * (a + 1)), a * (HD + 1) + HD
                    last = dve.memset(vals[rows, seqs, :, at:at + 1], 1.0)
                last.then_inc(vals_clear, 1)

            def mixture(layer):
                def weight_of(b, m):
                    if not isinstance(m, int):
                        return weights[:, b % 2, 1]
                    return weights[:, b % 2, m // HALF_SLABS] if m < EXPERT_SLABS else one[:]

                def add_sum(b):
                    dve.wait_ge(yT_done, NBLK * layer + b + 1)
                    xs = x[:, TPB * b:TPB * (b + 1), :].rearrange("p (k t) d -> p k (t d)", k=2)
                    dve.tensor_tensor(xs, xs, sum_bank(b), ALU.add).then_inc(y_added, 1)

                for b, first in blocks(layer):
                    def step(n, m, s):
                        q = s % 2
                        if isinstance(m, int) and m == 1 and b > 0:
                            add_sum(b - 1)
                        dve.wait_ge(silu_ready, n + 1)
                        if isinstance(m, int) and m == 0:
                            dve.wait_ge(weights_ready, NBLK * layer + b + 1)
                        dve.tensor_tensor(sgc[:, q], sg[:, q], weight_of(b, m), ALU.mult).then_inc(sgc_ready, 1)
                        dve.wait_ge(up_done, n + 1)
                        dve.wait_ge(sgc_ready, n + 1)
                        dve.tensor_tensor(h[:, q], sgc[:, q], bank[2 + q], ALU.mult).then_inc(h_ready, 1)
                        if preparation(layer, b, m):
                            prepare(*preparation(layer, b, m), m)
                        if isinstance(m, int) and 0 <= m - STATS_FROM < TPB and b + 2 < NBLK:
                            tile_stats(2 * layer + 1, TPB * (b + 2) + m - STATS_FROM)
                        if layer == 0 and isinstance(m, int) and m in (7, 9):
                            clear_values(PIECES * b + (m - 7) // 2)
                        dve.wait_ge(h_hi_ready, n + 1)
                        at_least(dve, down_done, n - 1)
                        dve.tensor_tensor(h_lo[:, q], h[:, q], h_hi[:, q].bitcast(F32), ALU.subtract) \
                           .then_inc(h_lo_ready, 1)

                    over_steps(dve, layer, first, step)
                if layer == 0:
                    norm_stats(2, 0)
                    for t in range(2):
                        normalise(2, t)
                add_sum(NBLK - 1)
                if layer == 0:
                    for t in range(TPB, TPB + 2):
                        tile_stats(2, t)
                dve.wait_ge(y_added, NBLK * (layer + 1))

            mixture(0)

            def heads(t):
                return probs[:, t % 2].rearrange("p (h k) -> p h k", h=HEADS)

            for i in range(NT + 2):
                if i < NT:
                    if i + TPB + 2 < NT:
                        tile_stats(2, i + TPB + 2)
                    if i + 2 < NT:
                        normalise(2, i + 2)
                    dve.wait_ge(s_done, i + 1)
                    at_least(dve, pT_done, i - 1)
                    src = psum[:, 4 + 2 * (i % 2):6 + 2 * (i % 2), :].rearrange("p k (h s) -> p (k h) s", s=S)
                    dve.scalar_tensor_tensor(out=heads(i), in0=src, scalar=HD ** -0.5,
                                             in1=floor[:].unsqueeze(1).broadcast_to([P, HEADS, S]),
                                             op0=ALU.mult, op1=ALU.max).then_inc(s_evac, 1)
                    dve.wait_ge(s_evac, i + 1)
                    dve.tensor_reduce(smax[:, i % 2], heads(i), AX, ALU.max).then_inc(smax_ready, 1)
                if i >= 2:
                    j = i - 2
                    dve.wait_ge(pv_done, j + 1)
                    o = bank[1][:, 0:PAIRS * VW].rearrange("p (h w) -> p h w", w=HD + 1)
                    chain(dve.reciprocal(orec[:, j % 2], o[:, :, HD]))
                    chain(dve.tensor_tensor(onorm[:, j % 2].rearrange("p (h d) -> p h d", d=HD), o[:, :, 0:HD],
                                            orec[:, j % 2].unsqueeze(2).broadcast_to([P, HEADS, HD]), ALU.mult))
                    dve.tensor_tensor(x[:, j, :], x[:, j, :], onorm[:, j % 2], ALU.add).then_inc(att_added, 1)
                if PREP_FROM[1] - TPB <= i < PREP_FROM[1] + TPB:
                    tile = i - (PREP_FROM[1] - TPB)
                    dve.wait_ge(att_added, tile + 1)
                    tile_stats(3, tile)
                if PREP_FROM[1] <= i:
                    prepare(3, 0, i - PREP_FROM[1])
            dve.wait_ge(att_added, NT)
            mixture(1)

        @block.tensor
        def _(pe):
            def transposes(ln, t):
                pe.wait_ge(xn_ready[ln], t + 1)
                if ln % 2 == 1 and t % TPB == 0:
                    at_least(pe, weights_ready, NBLK * (ln // 2) + t // TPB)
                at_least(pe, tr_evac[ln], t if ln else t - 3)
                for k in range(DK):
                    last = pe.transpose(tr_bank(ln, t)[:, P * k:P * (k + 1)],
                                        xn_of(ln, t)[:, P * k:P * (k + 1)], ident[:])
                last.then_inc(tr_done[ln], 1)

            def three(out, a, b, start, stop):
                pe.matmul(out, a[0], b[0], start=start, stop=False)
                pe.matmul(out, a[0], b[1], start=False, stop=False)
                return pe.matmul(out, a[1], b[0], start=False, stop=stop)

            def logits(ln, t):
                layer, j, i = ln // 2, t // TPB, t % TPB
                pe.wait_ge(tr_evac[ln], t + 1)
                tile = slice(P * i, P * (i + 1))
                out = logits_at(ln, j)[:, i]
                w = [router_parts[:, layer * DK + k] for k in range(DK)]
                pe.matmul(out, x_hi[:, j % 2, 0, tile], w[0], start=True, stop=False)
                for k in range(DK):
                    pe.matmul(out[:, 0], x_lo[:, j % 2, k, tile], w[k][:, 0], start=False, stop=False)
                last = pe.matmul(out, x_hi[:, j % 2, 1, tile], w[1], start=False, stop=True)
                if i == TPB - 1:
                    last.then_inc(logits_done, 1)

            def combine_weights(ln, j):
                pe.wait_ge(cwp_ready, NBLK * (ln // 2) + j + 1)
                for t in range(TPB):
                    last = pe.transpose(cwT_at(ln, j)[:, P * t:P * (t + 1)], cwp[:, t, :], identb[:])
                last.then_inc(cwT_done, 1)

            def spread_weights(ln, j):
                pe.wait_ge(cwT_evac, NBLK * (ln // 2) + j + 1)
                for g in range(E // HALF):
                    last = pe.matmul(bank[4 + g], sel[:, g, :], cwT[:], start=True, stop=True)
                last.then_inc(weights_done, 1)

            def prepare(ln, j, m):
                if 2 <= m < 2 + TPB:
                    logits(ln, TPB * j + m - 2)
                if 1 <= m < 1 + TPB:
                    transposes(ln, TPB * j + m - 1)
                if m == 11:
                    combine_weights(ln, j)
                if m == 12:
                    spread_weights(ln, j)

            def prepare_rest(ln, begin):
                for m in range(begin, PREP_STEPS):
                    prepare(ln, 0, m)

            pe.wait_ge(ident_in, 16)
            for t in range(NT):
                transposes(0, t)
                if t % TPB == TPB - 1:
                    j = t // TPB
                    pe.wait_ge(wh_in, 16)
                    pe.wait_ge(ctx_in[j], 16)
                    for hd in range(RH):
                        n = RH * j + hd
                        at_least(pe, k_evac, n - 1)
                        pe.matmul(bank[4 + n % 2], wh[:, hd, :], ctxT[:, hd, BLK * j:BLK * (j + 1)], start=True,
                                  stop=True).then_inc(k_done, 1)
            pe.wait_ge(tr_evac[0], NT)
            for n in range(RH * NBLK):
                hd, cols = n // NBLK, slice(BLK * (n % NBLK), BLK * (n % NBLK + 1))
                at_least(pe, q_evac, n - 1)
                pe.matmul(bank[2 + n % 2], wh[:, hd, :], xT[:, hd, cols], start=True, stop=True).then_inc(q_done, 1)
            pe.wait_ge(q_evac, RH * NBLK)
            pe.wait_ge(k_evac, RH * NBLK)
            for hd in range(RH):
                for b in range(B):
                    seq = slice(S * b, S * (b + 1))
                    last = pe.matmul(bank[6][0:S, S * hd:S * (hd + 1)], kT[:, hd, seq], qT[:, hd, seq],
                                     start=b == 0, stop=b == B - 1)
            last.then_inc(ret_scores, 1)

            def values_and_gate(i):
                tile = slice(P * i, P * (i + 1))
                for hd in range(RH):
                    last = pe.transpose(bank[3][:, P * hd:P * (hd + 1)], kT[:, hd, tile], ident[:])
                last.then_inc(v_done, 1)
                pe.wait_ge(attw_in, 16 * 6)
                at_least(pe, g_relu, i)
                for k in range(DK):
                    last = pe.matmul(bank[2][:, 0:D], xT[:, k, tile], wg[:, k, :], start=k == 0, stop=k == DK - 1)
                last.then_inc(g_done, 1)

            values_and_gate(0)
            pe.wait_ge(ret_attn, 1)
            pe.matmul(bank[7][:, 0:RH * S], dup, attn, start=True, stop=True).then_inc(ret_dup, 1)
            for i in range(NT + 4):
                if 1 <= i <= NT:
                    p = (i - 1) % 2
                    pe.wait_ge(v_evac, i)
                    pe.wait_ge(ret_diag, 1)
                    at_least(pe, wy_ready, i - 2)
                    for hd in range(RH):
                        last = pe.matmul(bank[p][:, P * hd:P * (hd + 1)], attn_diag[:, hd, :],
                                         vt[:, p, P * hd:P * (hd + 1)], start=True, stop=True)
                    last.then_inc(o_done, 1)
                if 0 < i < NT:
                    values_and_gate(i)
                if 3 <= i < NT + 3:
                    p = (i - 3) % 2
                    pe.wait_ge(wy_ready, i - 2)
                    at_least(pe, wyT_evac, i - 3)
                    for k in range(DK):
                        last = pe.transpose(bank[4][:, P * k:P * (k + 1)], wy[:, p, P * k:P * (k + 1)], ident[:])
                    last.then_inc(wyT_done, 1)
                if 4 <= i:
                    p = (i - 4) % 2
                    pe.wait_ge(wyT_evac, i - 3)
                    at_least(pe, x_added, i - 5)
                    for k in range(DK):
                        last = pe.matmul(bank[6 + p][:, 0:D], wyT[:, p, P * k:P * (k + 1)], wo[:, k, :],
                                         start=k == 0, stop=k == DK - 1)
                    last.then_inc(proj_done, 1)
                if PREP_FROM[0] < i:
                    prepare(1, 0, i - PREP_FROM[0] - 1)

            def mixture(layer):
                def sum_transposed(b):
                    pe.wait_ge(y_evac, NBLK * layer + b + 1)
                    for t in range(TPB):
                        for k in range(DK):
                            at = D * (t % 2) + P * k
                            last = pe.transpose(sum_bank(b)[:, t // 2, at:at + P], ysb[:, k, P * t:P * (t + 1)], ident[:])
                    last.then_inc(yT_done, 1)

                for b, first in blocks(layer):
                    def up(n, m, s):
                        q, r = s % 2, s % RAW
                        pe.wait_ge(up_split, n + 1)

                        def half(out, base):
                            for k in range(DK):
                                w = slice(base + P * k, base + P * (k + 1))
                                last = three(out, (w_hi[:, q, w], w_lo[:, q, w]),
                                             (x_hi[:, b % 2, k], x_lo[:, b % 2, k]), k == 0, k == DK - 1)
                            return last

                        if layer == 1 and b == 0 and isinstance(m, int) and m == 1:
                            pe.wait_ge(att_added, NT)
                        at_least(pe, silu_ready, n - 1)
                        half(bank[q], 0).then_inc(gate_done, 1)
                        if isinstance(m, int) and m == 1 and b > 0:
                            sum_transposed(b - 1)
                        if preparation(layer, b, m):
                            prepare(*preparation(layer, b, m), m)
                        at_least(pe, h_ready, n - 1)
                        half(bank[2 + q], DK * P).then_inc(up_done, 1)

                    def down(n, s, start, stop):
                        q = s % 2
                        pe.wait_ge(down_split, n + 1)
                        pe.wait_ge(h_lo_ready, n + 1)
                        for k in range(DK):
                            w = slice(2 * DK * P + P * k, 2 * DK * P + P * (k + 1))
                            last = three(bank[6 + k], (w_hi[:, q, w], w_lo[:, q, w]), (h_hi[:, q], h_lo[:, q]),
                                         start, stop)
                        last.then_inc(down_done, 1)

                    def step(n, m, s):
                        up(n, m, s)
                        if isinstance(m, int) and m == 1:
                            at_least(pe, y_added, NBLK * layer + b)
                        if not isinstance(m, int) or m > 0:
                            down(n - 1, s - 1, isinstance(m, int) and m == 1, False)
                        elif b > 0:
                            down(n - 1, s - 1, False, True)

                    over_steps(pe, layer, first, step)
                down(first + NM[layer] - 1, first + NM[layer] - 1, False, True)
                sum_transposed(NBLK - 1)

            prepare_rest(1, PREP_STEPS - 1)
            mixture(0)
            transposes(2, 0)
            for i in range(NT + 2):
                if i < NT:
                    p = i % 2
                    pe.wait_ge(keys_act, i + 1)
                    pe.wait_ge(keys_pool, i + 1)
                    pe.wait_ge(tr_evac[2], i + 1)
                    at_least(pe, s_evac, i - 1)
                    for g in range(DK):
                        out = bank[4 + 2 * p + g]
                        pe.matmul(out, identb[:], cbig[:], start=True, stop=False, skip_group_check=True)
                        for b in range(2):
                            q = slice(S * b, S * (b + 1))
                            last = pe.matmul(out[q], q_t[:, p, g, q],
                                             keys[:, p, g, b].rearrange("p h s -> p (h s)"), start=False, stop=True,
                                             skip_group_check=True)
                    last.then_inc(s_done, 1)
                at_least(pe, tr_evac[3], min(i - PREP_FROM[1] - 1, TPB))
                if i + 1 < NT:
                    transposes(2, i + 1)
                if 2 <= i - PREP_FROM[1] < 2 + TPB:
                    pe.wait_ge(att_added, i - 2)
                    logits(3, i - PREP_FROM[1] - 2)
                if i == NT + 1:
                    combine_weights(3, 0)
                if i >= 2:
                    j = i - 2
                    p = j % 2
                    pe.wait_ge(vals_ready, 2 * PIECES * NBLK)
                    pe.wait_ge(pT_evac, j + 1)
                    at_least(pe, att_added, j)
                    if i > PREP_FROM[1] + 5:
                        pe.wait_ge(z_ready, NBLK + 1)
                    for b in range(2):
                        for n in range(PAIRS):
                            q = slice(P * n + S * b, P * n + S * (b + 1))
                            last = pe.matmul(bank[1][S * b:S * (b + 1), VW * n:VW * (n + 1)], probsT[:, p, q],
                                             vals[:, 2 * j + b, n, :], start=True, stop=True)
                    last.then_inc(pv_done, 1)
                if 1 <= i - PREP_FROM[1] < 1 + TPB:
                    pe.wait_ge(tr_evac[2], min(i + 2, NT))
                    transposes(3, i - PREP_FROM[1] - 1)
                if 1 <= i <= NT:
                    j = i - 1
                    p = j % 2
                    pe.wait_ge(probs_ready, j + 1)
                    at_least(pe, pT_evac, j)
                    for n in range(PAIRS):
                        last = pe.transpose(bank[2 + n // 4][:, P * (n % 4):P * (n % 4 + 1)],
                                            probs[:, p, P * n:P * (n + 1)], ident[:])
                    last.then_inc(pT_done, 1)
            prepare_rest(3, PREP_STEPS - 1)
            mixture(1)


def masks():
    f = np.float32
    gam = (1.0 - f(2.0) ** (-5.0 - np.arange(RH, dtype=f))).astype(f)
    at = np.arange(S, dtype=f)
    expo = at[None, :] - at[:, None]
    decay = np.where(expo[None] <= 0, gam[:, None, None] ** expo[None], 0.0).astype(f)
    decay = decay / np.sqrt(decay.sum(axis=-1, dtype=f))[:, None, :] / np.sqrt(f(P))
    dmask = np.ascontiguousarray(decay.transpose(2, 0, 1).reshape(S, RH * S), f)
    eye = np.eye(S, dtype=f)
    chan = np.arange(P)
    head_mask = np.stack([(chan // HD == h) for h in range(HPH)], 1).astype(f)
    sel = np.zeros((P, E // HALF, P), f)
    for k in range(3):
        for g in range(E // HALF):
            sel[E * k + HALF * g + chan // ROWS, g, chan] = 1.0
    masked = np.arange(S)[None, :] > np.arange(S)[:, None]
    masked = np.tile(masked, (2, HPH))
    return {
        "identf": np.eye(P, dtype=f), "identb": np.eye(P, dtype=f), "dmask": dmask, "dup": np.hstack([eye, eye]),
        "head_mask": head_mask, "sel": sel, "cbig": np.where(masked, f(-2.0 ** 100), f(0.0)).astype(f),
        "floor": np.where(masked[:, 0:S], f(MASKED), f(-3.4e38)).astype(f),
    }


def by_slab(w):
    return w.reshape(E // HALF, HALF, HALF_SLABS, ROWS, D).transpose(0, 2, 1, 3, 4).reshape(E * HID, D)


def slabs(gate, up, down):
    n = gate.shape[0] // P
    parts = [w.reshape(n, P, DK, P).transpose(0, 3, 2, 1).reshape(n, P, DK * P) for w in (gate, up)]
    return np.ascontiguousarray(np.concatenate(parts + [down.reshape(n, P, D)], 2))


def kernel(**inputs):
    import concourse.bacc as bacc
    import ml_dtypes
    from concourse.bass_utils import run_bass_kernel_spmd

    a = {k: np.asarray(v) for k, v in inputs.items()}
    c = masks()
    for k in ("identb", "sel", "cbig"):
        c[k] = c[k].astype(ml_dtypes.bfloat16)
    ctx = a["ctx_2048"]
    pad = np.zeros((NM[1] * P - E * HID - SHARED, D), np.float32)
    up1, sh1 = a["L1_ffn_expert_up_w"], a["L1_ffn_shared_up_w"]
    arrays = {
        "x": a["x"].reshape(TOK, D),
        "ctxT": ctx.reshape(TOK, DK, P).transpose(2, 1, 0),
        "ctxV": ctx.reshape(B, S, PAIRS, 2, HD).transpose(3, 1, 0, 2, 4).reshape(P, DK * TOK),
        "wh": a["L0_xattn_Wh"].transpose(1, 0, 2),
        "wg": a["L0_xattn_wg_w"].reshape(DK, P, D).transpose(1, 0, 2),
        "wo": a["L0_xattn_wo_w"].reshape(DK, P, D).transpose(1, 0, 2),
        "gamma": np.broadcast_to(a["L0_xattn_gn_gamma"], (P, D)),
        "beta": np.broadcast_to(a["L0_xattn_gn_beta"], (P, D)),
        "router": np.stack([a["L0_ffn_gate_w"], a["L1_ffn_gate_w"]]).reshape(2, E, DK, P).transpose(3, 0, 2, 1)
                    .reshape(P, 2 * DK * E),
        "w0": slabs(by_slab(a["L0_ffn_w_gate"]), by_slab(a["L0_ffn_w_up"]),
                    by_slab(a["L0_ffn_w_down"].transpose(0, 2, 1))),
        "w1": slabs(np.concatenate([by_slab(up1[:, :HID]), sh1[:SHARED], pad]),
                    np.concatenate([by_slab(up1[:, HID:]), sh1[SHARED:], pad]),
                    np.concatenate([by_slab(a["L1_ffn_expert_down_w"].transpose(0, 2, 1)),
                                    a["L1_ffn_shared_down_w"].T, pad])),
        "sel": c["sel"], "identf": c["identf"], "identb": c["identb"], "dmask": c["dmask"], "dup": c["dup"],
        "head_mask": c["head_mask"], "cbig": c["cbig"], "floor": c["floor"],
    }
    arrays = {f"in_{k}": np.ascontiguousarray(v) for k, v in arrays.items()}
    nc = bacc.Bacc("TRN2", target_bir_lowering=False, num_devices=1)
    aps = [nc.dram_tensor(k, v.shape, mybir.dt.from_np(v.dtype), kind="ExternalInput").ap()
           for k, v in arrays.items()]
    out = nc.dram_tensor("out", (TOK, D), F32, kind="ExternalOutput").ap()
    retention_mixture_layers(nc, *aps, out)
    got = run_bass_kernel_spmd(nc, [arrays], core_ids=[0])
    return got.results[0]["out"].reshape(B, S, D)
```
